# Optimizing a Trainium2 kernel written in Bass

```python
import numpy as np
import jax
import jax.numpy as jnp

def _softmax(x, axis=-1):
    return jax.nn.softmax(x, axis=axis)

def _gelu(x):
    return jax.nn.gelu(x, approximate=True)

def _silu(x):
    return jax.nn.silu(x)

def _sigmoid(x):
    return jax.nn.sigmoid(x)

def _layernorm(x, axis=-1, eps=1e-05):
    m = jnp.mean(x, axis=axis, keepdims=True)
    v = jnp.var(x, axis=axis, keepdims=True)
    return (x - m) / jnp.sqrt(v + eps)

def _scatter_add(tgt, idx, src, axis=0):
    return tgt.at[idx].add(src)

def _segment_sum(src, seg, n):
    return jax.ops.segment_sum(src, seg, n)
kernel_name = 'mk_hybrid_d1_jaxref_r8_e1bbb4'

def setup_inputs(seed: int=0):
    np.random.seed(seed)
    _w = jnp.asarray

    def _L0_attn_a_setup():
        import jax, jax.numpy as jnp
        import numpy as np
        HEAD_NUM = 16
        key = jax.random.key(seed)
        ks = jax.random.split(key, 9)
        B, S, D = (4, 256, 128)

        def xavier(k, shape):
            limit = jnp.sqrt(6.0 / (shape[0] + shape[1]))
            return jax.random.uniform(k, shape, jnp.float32, -limit, limit)
        return {'x': jax.random.normal(ks[0], (B, S, D), jnp.float32), 'Wq': xavier(ks[1], (D, D)), 'bq': jnp.zeros((D,), jnp.float32), 'Wk': xavier(ks[2], (D, D)), 'bk': jnp.zeros((D,), jnp.float32), 'Wv': xavier(ks[3], (D, D)), 'bv': jnp.zeros((D,), jnp.float32), 'Wo': xavier(ks[4], (D, D)), 'bo': jnp.zeros((D,), jnp.float32)}
    _L0_attn_a_in = _L0_attn_a_setup()

    def _L0_attn_b_setup():
        import jax, jax.numpy as jnp
        import numpy as np
        import math
        EMBED_DIM = 128
        NHEAD = 16
        HEAD_DIM = 64
        BATCH = 2
        SEQ = 256
        key = jax.random.key(seed)
        k_in, k_wqkv, k_wo, k_g = jax.random.split(key, 4)
        std = math.sqrt(2.0 / EMBED_DIM)
        inputs = jax.random.normal(k_in, (BATCH, SEQ, EMBED_DIM), dtype=jnp.float32)
        Wqkv_w = jax.random.normal(k_wqkv, (3 * NHEAD * HEAD_DIM, EMBED_DIM), dtype=jnp.float32) * std
        Wqkv_b = jnp.zeros((3 * NHEAD * HEAD_DIM,), dtype=jnp.float32)
        Wo_w = jax.random.normal(k_wo, (EMBED_DIM, NHEAD * HEAD_DIM), dtype=jnp.float32) * std
        Wo_b = jnp.zeros((EMBED_DIM,), dtype=jnp.float32)
        ghost = jax.random.uniform(k_g, (NHEAD,), dtype=jnp.float32) * 0.1
        return {'inputs': inputs, 'Wqkv_w': Wqkv_w, 'Wqkv_b': Wqkv_b, 'Wo_w': Wo_w, 'Wo_b': Wo_b, 'ghost': ghost}
    _L0_attn_b_in = _L0_attn_b_setup()

    def _L0_ffn_setup():
        import jax, jax.numpy as jnp
        import numpy as np
        DIM = 128

        def _reference_tuple_inner(x, W_r, W_k, W_v, mu_r, mu_k):
            B, T, C = x.shape
            x_prev = jnp.concatenate([jnp.zeros((B, 1, C), x.dtype), x[:, :-1, :]], axis=1)
            xr = mu_r * x + (1.0 - mu_r) * x_prev
            xk = mu_k * x + (1.0 - mu_k) * x_prev
            r = jax.nn.sigmoid(jnp.einsum('btc,dc->btd', xr, W_r))
            k = jnp.einsum('btc,dc->btd', xk, W_k)
            k_act = jnp.square(jax.nn.relu(k))
            out = r * jnp.einsum('btc,dc->btd', k_act, W_v)
            new_state = x[:, -1, :]
            return (out, new_state)
        key = jax.random.key(seed)
        ks = jax.random.split(key, 6)
        B, T, C = (8, 256, DIM)
        x = jax.random.normal(ks[0], (B, T, C), dtype=jnp.float32)
        s = 1.0 / np.sqrt(C)
        W_r = jax.random.uniform(ks[1], (C, C), jnp.float32, -s, s)
        W_k = jax.random.uniform(ks[2], (C, C), jnp.float32, -s, s)
        W_v = jax.random.uniform(ks[3], (C, C), jnp.float32, -s, s)
        mu_r = jax.random.uniform(ks[4], (C,), jnp.float32)
        mu_k = jax.random.uniform(ks[5], (C,), jnp.float32)
        return {'x': x, 'W_r': W_r, 'W_k': W_k, 'W_v': W_v, 'mu_r': mu_r, 'mu_k': mu_k}
    _L0_ffn_in = _L0_ffn_setup()
    _d = {'L0_attn_a_x': _L0_attn_a_in['x'], 'L0_attn_a_Wq': _L0_attn_a_in['Wq'], 'L0_attn_a_bq': _L0_attn_a_in['bq'], 'L0_attn_a_Wk': _L0_attn_a_in['Wk'], 'L0_attn_a_bk': _L0_attn_a_in['bk'], 'L0_attn_a_Wv': _L0_attn_a_in['Wv'], 'L0_attn_a_bv': _L0_attn_a_in['bv'], 'L0_attn_a_Wo': _L0_attn_a_in['Wo'], 'L0_attn_a_bo': _L0_attn_a_in['bo'], 'L0_attn_b_Wqkv_w': _L0_attn_b_in['Wqkv_w'], 'L0_attn_b_Wqkv_b': _L0_attn_b_in['Wqkv_b'], 'L0_attn_b_Wo_w': _L0_attn_b_in['Wo_w'], 'L0_attn_b_Wo_b': _L0_attn_b_in['Wo_b'], 'L0_attn_b_ghost': _L0_attn_b_in['ghost'], 'L0_ffn_W_r': _L0_ffn_in['W_r'], 'L0_ffn_W_k': _L0_ffn_in['W_k'], 'L0_ffn_W_v': _L0_ffn_in['W_v'], 'L0_ffn_mu_r': _L0_ffn_in['mu_r'], 'L0_ffn_mu_k': _L0_ffn_in['mu_k']}
    _x0 = _d['L0_attn_a_x']
    _d['L0_attn_a_x'] = jax.random.normal(jax.random.fold_in(jax.random.key(seed), 1), (4, 512, 128), dtype=_x0.dtype)
    del _x0
    return _d

def reference(L0_attn_a_x, L0_attn_a_Wq, L0_attn_a_bq, L0_attn_a_Wk, L0_attn_a_bk, L0_attn_a_Wv, L0_attn_a_bv, L0_attn_a_Wo, L0_attn_a_bo, L0_attn_b_Wqkv_w, L0_attn_b_Wqkv_b, L0_attn_b_Wo_w, L0_attn_b_Wo_b, L0_attn_b_ghost, L0_ffn_W_r, L0_ffn_W_k, L0_ffn_W_v, L0_ffn_mu_r, L0_ffn_mu_k):

    def _L0_attn_a_ref(x, Wq, bq, Wk, bk, Wv, bv, Wo, bo):
        import jax, jax.numpy as jnp
        import numpy as np
        HEAD_NUM = 16
        B, S, D = x.shape
        H = HEAD_NUM
        hd = D // H

        def proj(W, b):
            return (x @ W.T + b).reshape(B, S, H, hd).transpose(0, 2, 1, 3)
        Q, K, V = (proj(Wq, bq), proj(Wk, bk), proj(Wv, bv))
        scale = 1.0 / jnp.sqrt(jnp.float32(hd))
        scores = jnp.einsum('bhqd,bhkd->bhqk', Q, K) * scale
        attn = jax.nn.softmax(scores, axis=-1)
        out = jnp.einsum('bhqk,bhkd->bhqd', attn, V)
        out = out.transpose(0, 2, 1, 3).reshape(B, S, D)
        return out @ Wo.T + bo

    def _L0_attn_b_ref(inputs, Wqkv_w, Wqkv_b, Wo_w, Wo_b, ghost):
        import jax, jax.numpy as jnp
        import numpy as np
        import math
        EMBED_DIM = 128
        NHEAD = 16
        HEAD_DIM = 64
        BATCH = 2
        SEQ = 256
        b, s, e = inputs.shape
        QKV = inputs @ Wqkv_w.T + Wqkv_b
        QKVh = QKV.reshape(b, s, 3, NHEAD, HEAD_DIM).transpose(0, 3, 2, 1, 4)
        Q, K, V = (QKVh[:, :, 0], QKVh[:, :, 1], QKVh[:, :, 2])
        scores = jnp.einsum('bhqd,bhkd->bhqk', Q, K) / math.sqrt(HEAD_DIM)
        row = jnp.arange(s)
        mask = jnp.where(row[None, :] > row[:, None], -jnp.inf, 0.0).astype(scores.dtype)
        scores = scores + mask[None, None]
        m = jnp.max(scores, axis=-1, keepdims=True)
        z = jnp.exp(scores - m)
        S = z / (jnp.sum(z, axis=-1, keepdims=True) + ghost.reshape(1, -1, 1, 1))
        A = jnp.einsum('bhqk,bhkd->bhqd', S, V)
        A = A.transpose(0, 2, 1, 3).reshape(b, s, NHEAD * HEAD_DIM)
        return A @ Wo_w.T + Wo_b

    def _L0_ffn_ref(x, W_r, W_k, W_v, mu_r, mu_k):
        import jax, jax.numpy as jnp
        import numpy as np
        DIM = 128

        def _reference_tuple_inner(x, W_r, W_k, W_v, mu_r, mu_k):
            B, T, C = x.shape
            x_prev = jnp.concatenate([jnp.zeros((B, 1, C), x.dtype), x[:, :-1, :]], axis=1)
            xr = mu_r * x + (1.0 - mu_r) * x_prev
            xk = mu_k * x + (1.0 - mu_k) * x_prev
            r = jax.nn.sigmoid(jnp.einsum('btc,dc->btd', xr, W_r))
            k = jnp.einsum('btc,dc->btd', xk, W_k)
            k_act = jnp.square(jax.nn.relu(k))
            out = r * jnp.einsum('btc,dc->btd', k_act, W_v)
            new_state = x[:, -1, :]
            return (out, new_state)
        return _reference_tuple_inner(x, W_r, W_k, W_v, mu_r, mu_k)[0]
    x = L0_attn_a_x
    x = x + _L0_attn_a_ref(_layernorm(x, axis=-1), L0_attn_a_Wq, L0_attn_a_bq, L0_attn_a_Wk, L0_attn_a_bk, L0_attn_a_Wv, L0_attn_a_bv, L0_attn_a_Wo, L0_attn_a_bo)
    x = x + _L0_ffn_ref(_layernorm(x, axis=-1), L0_ffn_W_r, L0_ffn_W_k, L0_ffn_W_v, L0_ffn_mu_r, L0_ffn_mu_k)
    x = x + _L0_attn_b_ref(_layernorm(x, axis=-1), L0_attn_b_Wqkv_w, L0_attn_b_Wqkv_b, L0_attn_b_Wo_w, L0_attn_b_Wo_b, L0_attn_b_ghost)
    x = x + _L0_ffn_ref(_layernorm(x, axis=-1), L0_ffn_W_r, L0_ffn_W_k, L0_ffn_W_v, L0_ffn_mu_r, L0_ffn_mu_k)
    return x

_drawn_inputs = setup_inputs


def setup_inputs(seed=0):
    import zlib

    import numpy as np

    out = dict(_drawn_inputs(seed))
    spreads = {'L0_attn_a_bq': (0.0, 0.319),
     'L0_attn_a_bk': (0.0, 0.8),
     'L0_attn_a_bv': (0.0, 0.1),
     'L0_attn_a_bo': (0.0, 0.1),
     'L0_attn_b_Wqkv_b': (0.0, 0.1),
     'L0_attn_b_Wo_b': (0.0, 0.1)}
    factors = {'L0_attn_b_ghost': 3.957, 'L0_ffn_mu_r': 3.544}
    for name, (base, spread) in spreads.items():
        noise = np.random.default_rng([zlib.crc32(name.encode()), seed]).standard_normal(out[name].shape)
        drawn = base * np.exp(spread * noise) if base else spread * noise
        out[name] = jnp.asarray(drawn.astype(out[name].dtype))
    for name, factor in factors.items():
        out[name] = (out[name] * factor).astype(out[name].dtype)
    return out
```

```python
from contextlib import ExitStack

import concourse.bass as bass
from concourse import mybir

F32 = mybir.dt.float32
F32R = mybir.dt.float32r
BF16 = mybir.dt.bfloat16
ALU = mybir.AluOpType
ACT = mybir.ActivationFunctionType
AX_X = mybir.AxisListType.X

P = 128
B = 4
S = 512
TILES = S // P
EPS = 1e-5

HEADS = 16
HD_A = P // HEADS
GROUP = 4
GROUPS = HEADS // GROUP
BLK = GROUP * HD_A
SCALE_A = HD_A ** -0.5
M_ROWS = 3 * BLK

HD_B = 64
PAIRS = HEADS // 2
SCALE_B = HD_B ** -0.5
CAUSAL = TILES * (TILES + 1) // 2 * P
ROW_AT = [P * i * (i + 1) // 2 for i in range(TILES + 1)]
COL_AT = [sum((TILES - k) * P for k in range(n)) for n in range(TILES + 1)]
UNITS = [(0,), (1,), (2, 3)]


def nth(b, per, n):
    return b * per + n


def each_batch(engine, batch):
    batch(0)
    with engine.Fori(1, B) as b:
        batch(b)


class Chip:

    def __init__(self, nc, ctx):
        self.nc, self.ctx = nc, ctx

    def sb(self, name, shape, dt=F32):
        return self.ctx.enter_context(self.nc.sbuf_tensor(name, shape, dt))

    def sems(self, *names):
        return [self.ctx.enter_context(self.nc.semaphore(n)) for n in names]


def memory(c):
    c.ps = c.ctx.enter_context(c.nc.psum_tensor("ps", [P, 8, 512], F32))
    c.x_res = c.sb("x_res", [P, B * TILES, P])
    c.ident = c.sb("ident", [P, P])
    c.ident_bf = c.sb("ident_bf", [P, P], BF16)
    c.causal_bf = c.sb("causal_bf", [P, P], BF16)
    c.head_mask = c.sb("head_mask", [P, GROUP])
    c.minus_half = c.sb("minus_half", [P, TILES])
    c.eps = c.sb("eps", [P, TILES])
    c.zero = c.sb("zero", [P, 1])
    c.ln_carry = c.sb("ln_carry", [P, 1])
    c.wqa_hi = c.sb("wqa_hi", [P, GROUPS, P], F32R)
    c.wqa_lo = c.sb("wqa_lo", [P, GROUPS, P], F32R)
    c.wka_hi = c.sb("wka_hi", [P, GROUPS, P], F32R)
    c.wka_lo = c.sb("wka_lo", [P, GROUPS, P], F32R)
    c.wva_hi = c.sb("wva_hi", [P, P], F32R)
    c.wva_lo = c.sb("wva_lo", [P, P], F32R)
    c.woa = c.sb("woa", [P, P])
    c.bqa = c.sb("bqa", [P, GROUPS])
    c.bka = c.sb("bka", [P, GROUPS])
    c.bva = c.sb("bva", [P, P])
    c.boa = c.sb("boa", [P, P])
    c.wb_hi = c.sb("wb_hi", [P, 3 * HEADS * HD_B], F32R)
    c.wb_lo = c.sb("wb_lo", [P, 3 * HEADS * HD_B], F32R)
    c.wob = c.sb("wob", [P, PAIRS, P])
    c.bqkb = c.sb("bqkb", [P, 2, PAIRS])
    c.bvb = c.sb("bvb", [P, HEADS * HD_B])
    c.bob = c.sb("bob", [P, P])
    c.ghost = c.sb("ghost", [P, HEADS])
    c.wr = c.sb("wr", [P, P])
    c.wk = c.sb("wk", [P, P])
    c.wv = c.sb("wv", [P, P])
    c.mu = c.sb("mu", [P, 2])
    c.stats = c.sb("stats", [P, TILES, 6])
    c.mean_var = c.sb("mean_var", [P, TILES, 2])
    c.var_eps = c.sb("var_eps", [P, TILES])
    c.rstd = c.sb("rstd", [P, TILES])
    c.xn = c.sb("xn", [P, TILES, P])
    c.xn_hi = c.sb("xn_hi", [P, S], F32R)
    c.xn_lo = c.sb("xn_lo", [P, S], F32R)
    c.v_a = c.sb("v_a", [P, TILES, HEADS, BLK])
    c.q_stack = c.sb("q_stack", [P, 3, S], F32R)
    c.k_group = c.sb("k_group", [P, S], F32R)
    c.stack = c.sb("stack", [P, 8, S], F32R)
    c.neg_max = c.sb("neg_max", [P, GROUP, TILES])
    c.max_cols = c.sb("max_cols", [P, TILES, BLK // 2, 2])
    c.probs = c.sb("probs", [P, 8, TILES * S])
    c.o_sb = c.sb("o_sb", [P, S])
    c.inv_a = c.sb("inv_a", [P, TILES, GROUP])
    c.a_tok = c.sb("a_tok", [P, TILES, P])
    c.a_chan = c.sb("a_chan", [P, S])
    c.v_b = c.sb("v_b", [P, TILES, HEADS * HD_B])
    c.neg_max_b = c.sb("neg_max_b", [P, HEADS, TILES])
    c.sum_b = c.sb("sum_b", [P, HEADS, TILES])
    c.den_b = c.sb("den_b", [P, 2, TILES])
    c.inv_b = c.sb("inv_b", [P, 2, TILES])
    c.inv_wide = c.sb("inv_wide", [P, TILES, 2, HD_B])
    c.inv_chan = c.sb("inv_chan", [P, S])
    c.xt = c.sb("xt", [P, S + 1])
    c.dx = c.sb("dx", [P, S])
    c.xr = c.sb("xr", [P, S])
    c.xk = c.sb("xk", [P, S])
    c.relu_k = c.sb("relu_k", [P, S])
    c.k_act = c.sb("k_act", [P, S])
    c.tanh_r = c.sb("tanh_r", [P, S])
    c.gated = c.sb("gated", [P, S])


def semaphores(c):
    c.x_loaded, c.wa_loaded, c.wb_loaded, c.const_loaded, c.wf_loaded, c.out_stored = c.sems(
        "x_loaded", "wa_loaded", "wb_loaded", "const_loaded", "wf_loaded", "out_stored")
    c.w_hi, c.w_lo, c.w_bf, c.set_zero = c.sems(
        "w_hi", "w_lo", "w_bf", "set_zero")
    c.ln_stats, c.ln_mean, c.ln_eps, c.ln_rstd, c.ln_xn, c.ln_turned = c.sems(
        "ln_stats", "ln_mean", "ln_eps", "ln_rstd", "ln_xn", "ln_turned")
    c.xn_hi_ok, c.xn_lo_ok, c.x_bias = c.sems(
        "xn_hi_ok", "xn_lo_ok", "x_bias")
    c.va_ps, c.va_ok, c.ka_ps, c.ka_hi, c.ka_lo, c.km_ok = c.sems(
        "va_ps", "va_ok", "ka_ps", "ka_hi", "ka_lo", "km_ok")
    c.qa_ps, c.qa_hi, c.qa_lo, c.n_ps, c.n_max, c.m_hi = c.sems(
        "qa_ps", "qa_hi", "qa_lo", "n_ps", "n_max", "m_hi")
    c.m_lo, c.m_turned, c.m_set, c.t_ps, c.t_exp, c.oa_ps = c.sems(
        "m_lo", "m_turned", "m_set", "t_ps", "t_exp", "oa_ps")
    c.oa_sb, c.oa_turned, c.oa_inv, c.oa_tok, c.at_turned, c.at_sb = c.sems(
        "oa_sb", "oa_turned", "oa_inv", "oa_tok", "at_turned", "at_sb")
    c.woa_ps, c.a_added = c.sems(
        "woa_ps", "a_added")
    c.vb_ps, c.vb_ok, c.qb_ps, c.qb_hi, c.qb_lo, c.kb_ps = c.sems(
        "vb_ps", "vb_ok", "qb_ps", "qb_hi", "qb_lo", "kb_ps")
    c.kb_hi, c.kb_lo, c.s_ps, c.s_max, c.s_exp, c.xp_ps = c.sems(
        "kb_hi", "kb_lo", "s_ps", "s_max", "s_exp", "xp_ps")
    c.xp_act, c.xp_dve, c.den_ok, c.inv_ok, c.wide_ok, c.inv_turned = c.sems(
        "xp_act", "xp_dve", "den_ok", "inv_ok", "wide_ok", "inv_turned")
    c.inv_sb, c.ob_ps, c.ob_sb, c.wob_ps, c.b_added = c.sems(
        "inv_sb", "ob_ps", "ob_sb", "wob_ps", "b_added")
    c.xt_ok, c.dx_ok, c.xr_ok, c.xk_ok, c.r_ps, c.k_ps = c.sems(
        "xt_ok", "dx_ok", "xr_ok", "xk_ok", "r_ps", "k_ps")
    c.r_tanh, c.k_relu, c.kact_ok, c.v_ps, c.gated_ok, c.f_added = c.sems(
        "r_tanh", "k_relu", "kact_ok", "v_ps", "gated_ok", "f_added")


def setup(c, d):
    nc = c.nc
    raw = c.probs[:].rearrange("p s n -> p (s n)")
    n_b = 3 * HEADS * HD_B
    raw_qa = raw[:, n_b:n_b + 512].rearrange("p (g n) -> p g n", g=GROUPS)
    raw_ka = raw[:, n_b + 512:n_b + 1024].rearrange("p (g n) -> p g n", g=GROUPS)
    raw_va = raw[:, n_b + 1024:n_b + 1152]
    raw_causal = raw[:, n_b + 1152:n_b + 1280]
    with nc.Block() as block:
        @block.sync
        def _(sp):
            for b in range(B):
                sp.dma_start(c.x_res[:, b * TILES:(b + 1) * TILES, :],
                             d["x"][b].rearrange("(t p) d -> p t d", p=P)).then_inc(c.x_loaded, 16)
            for dst, src in ((c.woa[:], d["woa"]), (c.bva[:], d["bva"].partition_broadcast(P)),
                             (c.boa[:], d["boa"].partition_broadcast(P)), (c.bqa[:], d["bqa"]),
                             (c.bka[:], d["bka"]), (c.wr[:], d["wr"]), (c.wk[:], d["wk"]), (c.wv[:], d["wv"]),
                             (c.mu[:], d["mu"]), (c.ghost[:], d["ghost"].partition_broadcast(P)),
                             (c.bob[:], d["bob"].partition_broadcast(P)),
                             (c.bvb[:], d["bvb"].partition_broadcast(P)), (c.bqkb[:], d["bqkb"]),
                             (c.wob[:], d["wob"].rearrange("(h p) d -> p h d", p=P))):
                sp.dma_start(dst, src).then_inc(c.wf_loaded, 16)
            sp.wait_ge(c.x_loaded, B * 16)
            sp.wait_ge(c.wf_loaded, 14 * 16)

        @block.scalar
        def _(act):
            act.dma_start(raw_qa, d["wqa"]).then_inc(c.wa_loaded, 16)
            act.dma_start(raw_ka, d["wka"]).then_inc(c.wa_loaded, 16)
            act.dma_start(raw_va, d["wva"]).then_inc(c.wa_loaded, 16)
            act.dma_start(raw[:, 0:n_b], d["wb"]).then_inc(c.wb_loaded, 16)
            for dst, src in ((c.ident[:], d["ident"]), (c.head_mask[:], d["head_mask"]),
                             (raw_causal, d["causal"])):
                act.dma_start(dst, src).then_inc(c.const_loaded, 16)
            act.wait_ge(c.const_loaded, 48)

        @block.vector
        def _(dve):
            dve.memset(c.v_a[:], 0.0).then_inc(c.set_zero, 1)
            dve.memset(c.max_cols[:], 0.0).then_inc(c.set_zero, 1)
            dve.memset(c.xt[:, 0:1], 0.0).then_inc(c.set_zero, 1)
            dve.memset(c.minus_half[:], -0.5).then_inc(c.set_zero, 1)
            dve.memset(c.eps[:], EPS).then_inc(c.set_zero, 1)
            dve.memset(c.zero[:], 0.0).then_inc(c.set_zero, 1)
            dve.wait_ge(c.set_zero, 1)
            dve.memset(c.v_a[:, :, :, HD_A:HD_A + 1], 1.0).then_inc(c.set_zero, 1)
            dve.wait_ge(c.wa_loaded, 48)
            n = 0
            for hi, lo, w in ((c.wqa_hi[:], c.wqa_lo[:], raw_qa), (c.wka_hi[:], c.wka_lo[:], raw_ka),
                              (c.wva_hi[:], c.wva_lo[:], raw_va)):
                dve.tensor_copy(hi, w).then_inc(c.w_hi, 1)
                n += 1
                dve.wait_ge(c.w_hi, n)
                dve.tensor_tensor(lo, w, hi.bitcast(F32), ALU.subtract).then_inc(c.w_lo, 1)
            dve.wait_ge(c.const_loaded, 48)
            dve.tensor_copy(c.ident_bf[:], c.ident[:]).then_inc(c.w_bf, 1)
            dve.tensor_copy(c.causal_bf[:], raw_causal).then_inc(c.w_bf, 1)
            dve.wait_ge(c.wb_loaded, 16)
            for at in range(0, n_b, 1024):
                w = raw[:, at:at + 1024]
                scale = SCALE_B if at == 0 else 1.0
                dve.tensor_scalar(c.wb_hi[:, at:at + 1024], w, scale, None, ALU.mult).then_inc(c.w_hi, 1)
                n += 1
                dve.wait_ge(c.w_hi, n)
                dve.scalar_tensor_tensor(out=c.wb_lo[:, at:at + 1024], in0=w, scalar=scale,
                                         in1=c.wb_hi[:, at:at + 1024].bitcast(F32),
                                         op0=ALU.mult, op1=ALU.subtract).then_inc(c.w_lo, 1)
            dve.wait_ge(c.w_lo, 6)
            dve.wait_ge(c.wf_loaded, 14 * 16)
            dve.tensor_scalar(c.bqkb[:, 0, :], c.bqkb[:, 0, :], SCALE_B, None, ALU.mult).then_inc(c.w_hi, 1)


def ln_vector(c, dve, l, b):
    k = l * B + b
    for t in range(TILES):
        dve.bn_stats(c.stats[:, t, :], c.x_res[:, bass.ds(b * TILES + t, 1), :]
                     .rearrange("p a d -> p (a d)")).then_inc(c.ln_stats, 1)
    dve.wait_ge(c.ln_eps, k)
    dve.wait_ge(c.ln_stats, nth(k, TILES, TILES))
    dve.memset(c.ln_carry[:], 0.0)
    for t in range(TILES):
        dve.bn_aggr(c.mean_var[:, t, :], c.stats[:, t, :]).then_inc(c.ln_mean, 1)
    dve.wait_ge(c.ln_rstd, k + 1)
    dve.wait_ge(c.ln_turned, k)
    for t in range(TILES):
        dve.tensor_scalar(c.xn[:, t, :], c.x_res[:, bass.ds(b * TILES + t, 1), :]
                          .rearrange("p a d -> p (a d)"), c.mean_var[:, t, 0:1], c.rstd[:, t:t + 1],
                          ALU.subtract, ALU.mult).then_inc(c.ln_xn, 1)


def ln_pool(c, pool, l, b):
    k = l * B + b
    pool.wait_ge(c.ln_mean, nth(k, TILES, TILES))
    pool.tensor_tensor(c.var_eps[:], c.mean_var[:, :, 1], c.eps[:], ALU.add).then_inc(c.ln_eps, 1)
    pool.wait_ge(c.ln_eps, k + 1)
    pool.wait_ge(c.ln_xn, nth(k, TILES, 0))
    pool.tensor_tensor(c.rstd[:], c.var_eps[:], c.minus_half[:], ALU.pow).then_inc(c.ln_rstd, 1)


def ln_tensor(c, pe, l, b, bank):
    k = l * B + b
    for t in range(TILES):
        pe.wait_ge(c.ln_xn, nth(k, TILES, t + 1))
        mm = pe.transpose(c.ps[:, bank, t * P:(t + 1) * P], c.xn[:, t, :], c.ident[:])
    mm.then_inc(c.ln_turned, 1)


def three_passes(pe, out, lhs, rhs, last_of_bank=True):
    (lh, ll), (rh, rl) = lhs, rhs
    pe.matmul(out, lh, rh, start=True, stop=False)
    pe.matmul(out, ll, rh, start=False, stop=False)
    return pe.matmul(out, lh, rl, start=False, stop=True)


def attention_a(c):
    nc, ps = c.nc, c.ps
    NB = GROUPS * GROUP * TILES
    TB = GROUPS * GROUP * 2

    def k_stack(g, j):
        return c.stack[:, GROUP * (g % 2) + j, :]

    def slot(g, j):
        return c.probs[:, GROUP * (g % 2) + j, :]

    with nc.Block() as block:
        @block.tensor
        def _(pe):
            def project(w_hi, w_lo, g, done):
                three_passes(pe, ps[:, 7, :], (w_hi[:, g, :], w_lo[:, g, :]), (c.xn_hi[:], c.xn_lo[:]))\
                    .then_inc(done, 1)

            def project_k(b, g):
                if g:
                    pe.wait_ge(c.oa_tok, nth(b, GROUPS, max(g - 3, 0)))
                    pe.wait_ge(c.m_set, nth(b, GROUPS, max(g - 1, 0)))
                else:
                    pe.wait_ge(c.va_ok, b + 1)
                project(c.wka_hi, c.wka_lo, g, c.ka_ps)

            def project_q(b, g):
                pe.wait_ge(c.ka_lo, nth(b, GROUPS, g + 1))
                project(c.wqa_hi, c.wqa_lo, g, c.qa_ps)

            def batch(b):
                pe.wait_ge(c.at_sb, b)
                ln_tensor(c, pe, 0, b, 7)
                pe.wait_ge(c.xn_lo_ok, b + 1)
                for t in range(TILES):
                    tok = slice(t * P, (t + 1) * P)
                    mm = three_passes(pe, ps[:, 7, tok], (c.xn_hi[:, tok], c.xn_lo[:, tok]),
                                      (c.wva_hi[:], c.wva_lo[:]))
                mm.then_inc(c.va_ps, 1)
                project_k(b, 0)
                project_q(b, 0)
                for s in range(GROUPS + 3):
                    for i in range(16 + 3):
                        if s < GROUPS and i < 16:
                            j, qt = divmod(i, TILES)
                            n = 16 * s + i
                            if qt == 0:
                                pe.wait_ge(c.km_ok, nth(b, HEADS, GROUP * s + j + 1))
                            if i == 0:
                                pe.wait_ge(c.qa_lo, nth(b, GROUPS, s + 1))
                            pe.wait_ge(c.n_max, nth(b, NB, max(n - 1, 0)))
                            pe.matmul(ps[:, n % 2, :], c.q_stack[:, s % 3, qt * P:(qt + 1) * P], k_stack(s, j),
                                      start=True, stop=True).then_inc(c.n_ps, 1)
                        if i == 1 and 0 <= s - 1 < GROUPS:
                            pe.wait_ge(c.qa_lo, nth(b, GROUPS, min(s + 1, GROUPS)))
                            pe.wait_ge(c.oa_tok, nth(b, GROUPS, max(s - 3, 0)))
                            pe.wait_ge(c.m_lo, nth(b, GROUPS, s))
                            for qt in range(TILES):
                                mm = pe.transpose(ps[0:BLK, 7, qt * P:(qt + 1) * P],
                                                  c.max_cols[:, qt, :, :].rearrange("p a b -> p (a b)"), c.ident[:])
                            mm.then_inc(c.m_turned, 1)
                        if i >= 3 and 0 <= s - 1 < GROUPS:
                            g = s - 1
                            j, kt = divmod(i - 3, TILES)
                            half = 8 * g + 2 * j + kt // 2
                            if i == 3:
                                pe.wait_ge(c.m_set, nth(b, GROUPS, g + 1))
                            if kt % 2 == 0:
                                pe.wait_ge(c.t_exp, nth(b, TB, max(half - 1, 0)))
                            mm = pe.matmul(ps[:, 2 + 2 * (half % 2) + kt % 2, :],
                                           k_stack(g, j)[:, kt * P:(kt + 1) * P], c.q_stack[:, g % 3, :],
                                           start=True, stop=True)
                            if kt % 2 == 1:
                                mm.then_inc(c.t_ps, 1)
                        if i == 4 and 0 <= s - 3 < GROUPS:
                            g = s - 3
                            if s - 1 < GROUPS:
                                pe.wait_ge(c.m_set, nth(b, GROUPS, s))
                            pe.wait_ge(c.oa_tok, nth(b, GROUPS, g))
                            pe.wait_ge(c.oa_sb, nth(b, GROUPS, g + 1))
                            for qt in range(TILES):
                                mm = pe.transpose(ps[:, 7, qt * P:(qt + 1) * P], c.o_sb[:, qt * P:(qt + 1) * P],
                                                  c.ident[:])
                            mm.then_inc(c.oa_turned, 1)
                        if i == 6 and s + 1 < GROUPS:
                            project_k(b, s + 1)
                        if i == 9 and s + 1 < GROUPS:
                            project_q(b, s + 1)
                        if i % 4 == 2 and i < 16 and 0 <= s - 2 < GROUPS:
                            g, kt = s - 2, i // 4
                            if kt == 0:
                                pe.wait_ge(c.va_ok, b + 1)
                                pe.wait_ge(c.t_exp, nth(b, TB, 8 * g + 8))
                                pe.wait_ge(c.oa_sb, nth(b, GROUPS, g))
                                if g == 0:
                                    pe.wait_ge(c.a_added, b)
                            for j in range(GROUP):
                                mm = pe.matmul(ps[BLK * j:BLK * (j + 1), 6, :], c.v_a[:, kt, GROUP * g + j, :],
                                               slot(g, j)[:, kt * S:(kt + 1) * S], start=(kt == 0),
                                               stop=(kt == TILES - 1))
                            if kt == TILES - 1:
                                mm.then_inc(c.oa_ps, 1)
                pe.wait_ge(c.oa_tok, nth(b, GROUPS, GROUPS))
                for t in range(TILES):
                    mm = pe.transpose(ps[:, 7, t * P:(t + 1) * P], c.a_tok[:, t, :], c.ident[:])
                mm.then_inc(c.at_turned, 1)
                pe.wait_ge(c.at_sb, b + 1)
                for t in range(TILES):
                    mm = pe.matmul(ps[:, 6, t * P:(t + 1) * P], c.a_chan[:, t * P:(t + 1) * P], c.woa[:],
                                   start=True, stop=True)
                mm.then_inc(c.woa_ps, 1)

            each_batch(pe, batch)

        @block.vector
        def _(dve):
            def k_low(b, g):
                rows = slice(BLK, 2 * BLK)
                dve.wait_ge(c.ka_hi, nth(b, GROUPS, g + 1))
                dve.scalar_tensor_tensor(out=c.k_group[rows, :], in0=ps[rows, 7, :], scalar=c.bka[rows, g:g + 1],
                                         in1=c.k_group[rows, :].bitcast(F32), op0=ALU.add, op1=ALU.subtract)\
                   .then_inc(c.ka_lo, 1)

            def q_low(b, g):
                rows = slice(2 * BLK, 3 * BLK)
                dve.wait_ge(c.qa_hi, nth(b, GROUPS, g + 1))
                dve.scalar_tensor_tensor(out=c.q_stack[rows, g % 3, :], in0=ps[rows, 7, :],
                                         scalar=c.bqa[rows, g:g + 1], in1=c.q_stack[rows, g % 3, :].bitcast(F32),
                                         op0=ALU.add, op1=ALU.subtract).then_inc(c.qa_lo, 1)

            def mask_keys(b, g, j):
                if j == 0:
                    dve.wait_ge(c.ka_lo, nth(b, GROUPS, g + 1))
                dve.wait_ge(c.t_ps, nth(b, TB, max(8 * (g - 2) + 2 * j + 2, 0)))
                dve.tensor_scalar(k_stack(g, j), c.k_group[:].bitcast(F32), c.head_mask[:, j:j + 1], None,
                                  ALU.mult).then_inc(c.km_ok, 1)

            def batch(b):
                ln_vector(c, dve, 0, b)
                dve.wait_ge(c.xn_hi_ok, b + 1)
                dve.tensor_tensor(c.xn_lo[:], ps[:, 7, :], c.xn_hi[:].bitcast(F32), ALU.subtract)\
                   .then_inc(c.xn_lo_ok, 1)
                dve.wait_ge(c.va_ps, b + 1)
                dve.wait_ge(c.oa_ps, nth(b, GROUPS, 0))
                dve.tensor_tensor(c.v_a[:, :, :, 0:HD_A],
                                  ps[:, 7, :].rearrange("p (t h d) -> p t h d", t=TILES, h=HEADS),
                                  c.bva[:].rearrange("p (a h d) -> p a h d", a=1, h=HEADS)
                                  .broadcast_to([P, TILES, HEADS, HD_A]), ALU.add).then_inc(c.va_ok, 1)
                k_low(b, 0)
                for j in range(GROUP):
                    mask_keys(b, 0, j)
                q_low(b, 0)
                for s in range(GROUPS + 3):
                    for j in range(GROUP):
                        if s < GROUPS:
                            for qt in range(TILES):
                                n = 16 * s + TILES * j + qt
                                dve.wait_ge(c.n_ps, nth(b, NB, n + 1))
                                if j == 0 and qt == 0:
                                    dve.wait_ge(c.m_lo, nth(b, GROUPS, s))
                                dve.tensor_reduce(c.neg_max[:, j, qt:qt + 1], ps[:, n % 2, :], AX_X, ALU.max,
                                                  negate=True).then_inc(c.n_max, 1)
                        if s + 1 < GROUPS:
                            if j == 1:
                                k_low(b, s + 1)
                            if j == 2:
                                q_low(b, s + 1)
                                mask_keys(b, s + 1, 0)
                        if j == 1 and 0 <= s - 3 < GROUPS:
                            g = s - 3
                            o = ps[:, 7, :].rearrange("p (t j d) -> p t j d", t=TILES, j=GROUP)
                            dve.wait_ge(c.oa_turned, nth(b, GROUPS, g + 1))
                            dve.reciprocal(c.inv_a[:], o[:, :, :, HD_A]).then_inc(c.oa_inv, 1)
                            dve.wait_ge(c.oa_inv, nth(b, GROUPS, g + 1))
                            if g == 0:
                                dve.wait_ge(c.at_turned, b)
                            dve.tensor_tensor(
                                c.a_tok[:, :, BLK * g:BLK * (g + 1)].rearrange("p t (j d) -> p t j d", j=GROUP),
                                o[:, :, :, 0:HD_A],
                                c.inv_a[:].rearrange("p t (j a) -> p t j a", a=1)
                                .broadcast_to([P, TILES, GROUP, HD_A]), ALU.mult).then_inc(c.oa_tok, 1)
                    if s < GROUPS:
                        nm = c.neg_max[:].rearrange("p j t -> p t j")
                        dve.wait_ge(c.n_max, nth(b, NB, 16 * s + 16))
                        dve.wait_ge(c.m_turned, nth(b, GROUPS, s))
                        dve.tensor_copy(c.max_cols[:, :, 0:GROUP, 0].bitcast(F32R), nm).then_inc(c.m_hi, 1)
                        dve.wait_ge(c.m_hi, nth(b, GROUPS, s + 1))
                        dve.tensor_tensor(c.max_cols[:, :, 0:GROUP, 1], nm, c.max_cols[:, :, 0:GROUP, 0],
                                          ALU.subtract).then_inc(c.m_lo, 1)
                    if s + 1 < GROUPS:
                        for j in range(1, GROUP):
                            mask_keys(b, s + 1, j)
                dve.wait_ge(c.woa_ps, b + 1)
                dve.wait_ge(c.x_bias, b + 1)
                x_b = c.x_res[:, bass.ds(b * TILES, TILES), :]
                dve.tensor_tensor(x_b, ps[:, 6, :].rearrange("p (t d) -> p t d", t=TILES), x_b, ALU.add)\
                   .then_inc(c.a_added, 1)

            each_batch(dve, batch)

        @block.scalar
        def _(act):
            def k_high(b, g):
                act.wait_ge(c.ka_ps, nth(b, GROUPS, g + 1))
                act.wait_ge(c.km_ok, nth(b, HEADS, GROUP * g))
                act.activation(c.k_group[:], ps[:, 7, :], ACT.Identity, bias=c.bka[:, g:g + 1])\
                   .then_inc(c.ka_hi, 1)

            def q_high(b, g):
                act.wait_ge(c.qa_ps, nth(b, GROUPS, g + 1))
                act.wait_ge(c.t_ps, nth(b, TB, max(8 * (g - 2), 0)))
                act.activation(c.q_stack[:, g % 3, :], ps[:, 7, :], ACT.Identity, bias=c.bqa[:, g:g + 1])\
                   .then_inc(c.qa_hi, 1)

            def batch(b):
                act.wait_ge(c.ln_turned, b + 1)
                act.wait_ge(c.qa_ps, nth(b, GROUPS, 0))
                act.activation(c.xn_hi[:], ps[:, 7, :], ACT.Copy).then_inc(c.xn_hi_ok, 1)
                k_high(b, 0)
                q_high(b, 0)
                for s in range(GROUPS + 3):
                    if 0 <= s - 1 < GROUPS:
                        act.wait_ge(c.m_turned, nth(b, GROUPS, s))
                        act.activation(c.q_stack[M_ROWS:P, (s - 1) % 3, :], ps[0:BLK, 7, :], ACT.Copy)\
                           .then_inc(c.m_set, 1)
                    for j in range(GROUP):
                        if 0 <= s - 1 < GROUPS:
                            g = s - 1
                            for h in range(2):
                                half = 8 * g + 2 * j + h
                                act.wait_ge(c.t_ps, nth(b, TB, half + 1))
                                if half % 8 == 0:
                                    act.wait_ge(c.oa_ps, nth(b, GROUPS, max(g - 1, 0)))
                                at = 2 + 2 * (half % 2)
                                act.activation(slot(g, j)[:, 2 * h * S:(2 * h + 2) * S]
                                               .rearrange("p (k n) -> p k n", k=2), ps[:, at:at + 2, :],
                                               ACT.Exp, scale=SCALE_A).then_inc(c.t_exp, 1)
                        if s + 1 < GROUPS:
                            if j == 0:
                                k_high(b, s + 1)
                            if j == 1:
                                q_high(b, s + 1)
                    if 0 <= s - 2 < GROUPS:
                        act.wait_ge(c.oa_ps, nth(b, GROUPS, s - 1))
                        act.wait_ge(c.oa_turned, nth(b, GROUPS, s - 2))
                        act.activation(c.o_sb[:], ps[:, 6, :], ACT.Copy).then_inc(c.oa_sb, 1)
                act.wait_ge(c.at_turned, b + 1)
                act.wait_ge(c.woa_ps, b)
                act.activation(c.a_chan[:], ps[:, 7, :], ACT.Copy).then_inc(c.at_sb, 1)

            each_batch(act, batch)

        @block.gpsimd
        def _(pool):
            def batch(b):
                ln_pool(c, pool, 0, b)
                add_bias(c, pool, 0, b, c.boa)

            each_batch(pool, batch)


def add_bias(c, pool, l, b, bias):
    pool.wait_ge(c.ln_xn, nth(l * B + b, TILES, TILES))
    x_b = c.x_res[:, bass.ds(b * TILES, TILES), :]
    pool.tensor_tensor(x_b, x_b, bias[:].rearrange("p (a d) -> p a d", a=1).broadcast_to([P, TILES, P]),
                       ALU.add).then_inc(c.x_bias, 1)


def attention_b(c):
    nc, ps = c.nc, c.ps
    SB_ = HEADS * TILES
    p_ring, pt_ring = 3, 4

    def part(p, which):
        return c.stack[:, 4 * (p % 2) + which, :]

    flat = c.probs[:].rearrange("p s n -> p (s n)")

    def p_at(h):
        at = 4 * TILES * S + (h % p_ring) * CAUSAL
        return flat[:, at:at + CAUSAL]

    def pt_at(h):
        at = (h % pt_ring) * TILES * S
        return flat[:, at:at + CAUSAL]

    def out_at(p):
        at = 6 * TILES * S + p * S
        return flat[:, at:at + S]

    def x_index(h, u):
        return 3 * h + u + h // 2

    X_BATCH = 3 * HEADS + PAIRS
    kinds = {}
    for h in range(HEADS):
        for u in range(3):
            kinds[x_index(h, u)] = "act" if u == 0 else "dve"
        if h % 2:
            kinds[x_index(h, 2) + 1] = "inv"

    def x_free(eng, b, x):
        y = x - 2
        if y < 0:
            eng.wait_ge(c.xp_dve, nth(b, 2 * HEADS, 0))
            eng.wait_ge(c.inv_sb, nth(b, PAIRS, 0))
            return
        kind = kinds[y]
        count = sum(1 for z in range(y + 1) if kinds[z] == kind)
        sem, per = {"act": (c.xp_act, HEADS), "dve": (c.xp_dve, 2 * HEADS), "inv": (c.inv_sb, PAIRS)}[kind]
        eng.wait_ge(sem, nth(b, per, count))

    with nc.Block() as block:
        @block.tensor
        def _(pe):
            def project(p, which, bank, done):
                col = which * HEADS * HD_B + p * P
                three_passes(pe, ps[:, bank, :], (c.wb_hi[:, col:col + P], c.wb_lo[:, col:col + P]),
                             (c.xn_hi[:], c.xn_lo[:])).then_inc(done, 1)

            def project_q(b, p):
                pe.wait_ge(c.qb_lo, nth(b, PAIRS, p))
                if p == 0:
                    pe.wait_ge(c.b_added, b)
                project(p, 0, 6, c.qb_ps)

            def project_k(b, p):
                pe.wait_ge(c.kb_lo, nth(b, PAIRS, p))
                project(p, 1, 7, c.kb_ps)

            def values(b, p):
                for kt in range(TILES):
                    for a in range(2):
                        h = 2 * p + a
                        if kt == 0 and a == 0:
                            pe.wait_ge(c.vb_ok, nth(b, 2 * TILES, 2 * TILES))
                            pe.wait_ge(c.ob_sb, nth(b, PAIRS, p))
                            pe.wait_ge(c.xp_act, nth(b, HEADS, h + 2))
                            pe.wait_ge(c.xp_dve, nth(b, 2 * HEADS, 2 * h + 4))
                        w = (TILES - kt) * P
                        mm = pe.matmul(ps[HD_B * a:HD_B * (a + 1), 5, kt * P:S],
                                       c.v_b[:, kt, h * HD_B:(h + 1) * HD_B],
                                       pt_at(h)[:, COL_AT[kt]:COL_AT[kt] + w],
                                       start=(kt == 0), stop=(kt == TILES - 1))
                mm.then_inc(c.ob_ps, 1)

            def batch(b):
                pe.wait_ge(c.kb_lo, nth(b, PAIRS, 0))
                ln_tensor(c, pe, 2, b, 7)
                pe.wait_ge(c.xn_lo_ok, B + b + 1)
                project_q(b, 0)
                project_k(b, 0)
                pe.wait_ge(c.kb_lo, nth(b, PAIRS, 1))
                for t in range(TILES):
                    for half in range(2):
                        n = 2 * t + half
                        tok = slice(t * P, (t + 1) * P)
                        col = 2 * HEADS * HD_B + half * S
                        bank = 7 if n % 2 else 4
                        if n > 1:
                            pe.wait_ge(c.vb_ok, nth(b, 2 * TILES, n - 1))
                        elif n == 0:
                            pe.wait_ge(c.xp_dve, nth(b, 2 * HEADS, 0))
                            pe.wait_ge(c.inv_sb, nth(b, PAIRS, 0))
                        three_passes(pe, ps[:, bank, :], (c.xn_hi[:, tok], c.xn_lo[:, tok]),
                                     (c.wb_hi[:, col:col + S], c.wb_lo[:, col:col + S])).then_inc(c.vb_ps, 1)
                pe.wait_ge(c.vb_ok, nth(b, 2 * TILES, 2 * TILES))
                for h in range(HEADS + 1):
                    p, a = divmod(h, 2)
                    rows = slice(HD_B * a, HD_B * (a + 1))
                    if a == 0 and p + 1 < PAIRS:
                        project_q(b, p + 1)
                    for i in range(TILES):
                        if h < HEADS:
                            n = TILES * h + i
                            w = (i + 1) * P
                            out = ps[:, n % 3, 0:w]
                            q = slice(i * P, (i + 1) * P)
                            if i == 0 and a == 0:
                                pe.wait_ge(c.qb_lo, nth(b, PAIRS, p + 1))
                                pe.wait_ge(c.kb_lo, nth(b, PAIRS, p + 1))
                            pe.wait_ge(c.s_exp, nth(b, SB_, max(n - 2, 0)))
                            pe.matmul(out, part(p, 0)[rows, q], part(p, 2)[rows, 0:w], start=True, stop=False)
                            pe.matmul(out, part(p, 1)[rows, q], part(p, 2)[rows, 0:w], start=False, stop=False)
                            pe.matmul(out, part(p, 0)[rows, q], part(p, 3)[rows, 0:w], start=False, stop=False)
                            pe.matmul(ps[:, n % 3, i * P:w], c.ident_bf[:], c.causal_bf[:], start=False, stop=True)\
                              .then_inc(c.s_ps, 1)
                        if h > 0 and i < 3:
                            x = x_index(h - 1, i)
                            x_free(pe, b, x)
                            if i == 0:
                                pe.wait_ge(c.s_exp, nth(b, SB_, TILES * h))
                            col = 0
                            for kt in UNITS[i]:
                                for qt in range(kt, TILES):
                                    at = ROW_AT[qt] + kt * P
                                    mm = pe.transpose(ps[:, 3 + x % 2, col:col + P], p_at(h - 1)[:, at:at + P],
                                                      c.ident[:])
                                    col += P
                            mm.then_inc(c.xp_ps, 1)
                    if a == 0 and h > 0:
                        x = x_index(h - 1, 2) + 1
                        x_free(pe, b, x)
                        pe.wait_ge(c.wide_ok, nth(b, PAIRS, p))
                        for qt in range(TILES):
                            mm = pe.transpose(ps[:, 3 + x % 2, qt * P:(qt + 1) * P],
                                              c.inv_wide[:, qt, :, :].rearrange("p a d -> p (a d)"), c.ident[:])
                        mm.then_inc(c.inv_turned, 1)
                        values(b, p - 1)
                    if a == 0 and p + 1 < PAIRS:
                        project_k(b, p + 1)
                pe.wait_ge(c.ob_sb, nth(b, PAIRS, PAIRS))
                for t in range(TILES):
                    for p in range(PAIRS):
                        mm = pe.matmul(ps[:, 6, t * P:(t + 1) * P], out_at(p)[:, t * P:(t + 1) * P],
                                       c.wob[:, p, :], start=(p == 0), stop=(p == PAIRS - 1))
                mm.then_inc(c.wob_ps, 1)

            each_batch(pe, batch)

        @block.vector
        def _(dve):
            def low(p, which, bank, hi_ready, b, done):
                dve.wait_ge(hi_ready, nth(b, PAIRS, p + 1))
                dve.scalar_tensor_tensor(out=part(p, 2 * which + 1), in0=ps[:, bank, :],
                                         scalar=c.bqkb[:, which, p:p + 1], in1=part(p, 2 * which).bitcast(F32),
                                         op0=ALU.add, op1=ALU.subtract).then_inc(done, 1)

            def q_low(b, p):
                low(p, 0, 6, c.qb_hi, b, c.qb_lo)

            def k_low(b, p):
                low(p, 1, 7, c.kb_hi, b, c.kb_lo)

            def finish(b, p):
                dve.wait_ge(c.ob_ps, nth(b, PAIRS, p + 1))
                dve.wait_ge(c.inv_sb, nth(b, PAIRS, p + 1))
                if p == 0:
                    dve.wait_ge(c.wob_ps, b)
                dve.tensor_tensor(out_at(p), ps[:, 5, :], c.inv_chan[:], ALU.mult).then_inc(c.ob_sb, 1)

            def batch(b):
                ln_vector(c, dve, 2, b)
                dve.wait_ge(c.xn_hi_ok, B + b + 1)
                dve.tensor_tensor(c.xn_lo[:], ps[:, 7, :], c.xn_hi[:].bitcast(F32), ALU.subtract)\
                   .then_inc(c.xn_lo_ok, 1)
                q_low(b, 0)
                k_low(b, 0)
                for n in range(2 * TILES):
                    t, half = divmod(n, 2)
                    dve.wait_ge(c.vb_ps, nth(b, 2 * TILES, n + 1))
                    if n == 0:
                        dve.wait_ge(c.ob_ps, nth(b, PAIRS, 0))
                    dve.tensor_tensor(c.v_b[:, t, half * S:(half + 1) * S], ps[:, 7 if n % 2 else 4, :],
                                      c.bvb[:, half * S:(half + 1) * S], ALU.add).then_inc(c.vb_ok, 1)
                for h in range(HEADS + 1):
                    p, a = divmod(h, 2)
                    for i in range(TILES):
                        if h < HEADS:
                            n = TILES * h + i
                            dve.wait_ge(c.s_ps, nth(b, SB_, n + 1))
                            dve.wait_ge(c.s_exp, nth(b, SB_, 0))
                            dve.tensor_reduce(c.neg_max_b[:, h, i:i + 1], ps[:, n % 3, 0:(i + 1) * P], AX_X,
                                              ALU.max, negate=True).then_inc(c.s_max, 1)
                        if a == 0 and i == 0 and p + 1 < PAIRS:
                            q_low(b, p + 1)
                        if h > 0 and 1 <= i < 3:
                            col, w = COL_AT[UNITS[i][0]], sum(TILES - k for k in UNITS[i]) * P
                            x = x_index(h - 1, i)
                            dve.wait_ge(c.xp_ps, nth(b, 3 * HEADS, 3 * (h - 1) + i + 1))
                            dve.wait_ge(c.ob_ps, nth(b, PAIRS, max((h - 1) // 2 - 1, 0)))
                            dve.tensor_copy(pt_at(h - 1)[:, col:col + w], ps[:, 3 + x % 2, 0:w])\
                               .then_inc(c.xp_dve, 1)
                    if a == 0 and p + 1 < PAIRS:
                        k_low(b, p + 1)
                    if a == 1:
                        dve.wait_ge(c.s_exp, nth(b, SB_, TILES * (h + 1)))
                        dve.wait_ge(c.wide_ok, nth(b, PAIRS, p))
                        dve.tensor_tensor(c.den_b[:], c.sum_b[:, 2 * p:2 * p + 2, :],
                                          c.ghost[:, 2 * p:2 * p + 2].rearrange("p (a b) -> p a b", b=1)
                                          .broadcast_to([P, 2, TILES]), ALU.add).then_inc(c.den_ok, 1)
                        dve.wait_ge(c.den_ok, nth(b, PAIRS, p + 1))
                        dve.reciprocal(c.inv_b[:], c.den_b[:]).then_inc(c.inv_ok, 1)
                        if p >= 1:
                            finish(b, p - 1)
                finish(b, PAIRS - 1)
                dve.wait_ge(c.wob_ps, b + 1)
                dve.wait_ge(c.x_bias, B + b + 1)
                x_b = c.x_res[:, bass.ds(b * TILES, TILES), :]
                dve.tensor_tensor(x_b, ps[:, 6, :].rearrange("p (t d) -> p t d", t=TILES), x_b, ALU.add)\
                   .then_inc(c.b_added, 1)

            each_batch(dve, batch)

        @block.scalar
        def _(act):
            def high(p, which, bank, ps_ready, b, done):
                act.wait_ge(ps_ready, nth(b, PAIRS, p + 1))
                act.wait_ge(c.s_ps, nth(b, SB_, max(2 * TILES * (p - 1), 0)))
                act.activation(part(p, 2 * which), ps[:, bank, :], ACT.Identity, bias=c.bqkb[:, which, p:p + 1])\
                   .then_inc(done, 1)

            def q_high(b, p):
                high(p, 0, 6, c.qb_ps, b, c.qb_hi)

            def k_high(b, p):
                high(p, 1, 7, c.kb_ps, b, c.kb_hi)

            def inv_rows(b, p):
                x = x_index(2 * p + 1, 2) + 1
                act.wait_ge(c.inv_turned, nth(b, PAIRS, p + 1))
                act.wait_ge(c.ob_sb, nth(b, PAIRS, p))
                act.activation(c.inv_chan[:], ps[:, 3 + x % 2, :], ACT.Copy).then_inc(c.inv_sb, 1)

            def batch(b):
                act.wait_ge(c.ln_turned, 2 * B + b + 1)
                act.wait_ge(c.vb_ps, nth(b, 2 * TILES, 0))
                act.wait_ge(c.kb_ps, nth(b, PAIRS, 0))
                act.activation(c.xn_hi[:], ps[:, 7, :], ACT.Copy).then_inc(c.xn_hi_ok, 1)
                q_high(b, 0)
                k_high(b, 0)
                for h in range(HEADS + 1):
                    p, a = divmod(h, 2)
                    for i in range(TILES):
                        if h < HEADS:
                            n = TILES * h + i
                            w = (i + 1) * P
                            act.wait_ge(c.s_max, nth(b, SB_, n + 1))
                            if i == 0:
                                act.wait_ge(c.xp_ps, nth(b, 3 * HEADS, max(3 * (h - p_ring + 1), 0)))
                                act.wait_ge(c.den_ok, nth(b, PAIRS, 0))
                            act.activation(p_at(h)[:, ROW_AT[i]:ROW_AT[i] + w], ps[:, n % 3, 0:w], ACT.Exp,
                                           bias=c.neg_max_b[:, h, i:i + 1], accum_out=c.sum_b[:, h, i:i + 1])\
                               .then_inc(c.s_exp, 1)
                        if a == 0 and i == 0 and p + 1 < PAIRS:
                            q_high(b, p + 1)
                        if h > 0 and i == 0:
                            x = x_index(h - 1, 0)
                            act.wait_ge(c.xp_ps, nth(b, 3 * HEADS, 3 * (h - 1) + 1))
                            act.wait_ge(c.ob_ps, nth(b, PAIRS, max((h - 1) // 2 - 1, 0)))
                            act.activation(pt_at(h - 1)[:, 0:S], ps[:, 3 + x % 2, :], ACT.Copy).then_inc(c.xp_act, 1)
                    if a == 0 and h > 0:
                        inv_rows(b, p - 1)
                    if a == 0 and p + 1 < PAIRS:
                        k_high(b, p + 1)

            each_batch(act, batch)

        @block.gpsimd
        def _(pool):
            def batch(b):
                ln_pool(c, pool, 2, b)
                add_bias(c, pool, 2, b, c.bob)
                for p in range(PAIRS):
                    pool.wait_ge(c.inv_ok, nth(b, PAIRS, p + 1))
                    pool.wait_ge(c.inv_turned, nth(b, PAIRS, p))
                    pool.tensor_tensor(c.inv_wide[:], c.inv_b[:].rearrange("p a (t d) -> p t a d", d=1)
                                       .broadcast_to([P, TILES, 2, HD_B]),
                                       c.zero[:].rearrange("p (a b d) -> p a b d", a=1, b=1)
                                       .broadcast_to([P, TILES, 2, HD_B]), ALU.add).then_inc(c.wide_ok, 1)

            each_batch(pool, batch)


def channel_mixing(c, f, out):
    nc, ps = c.nc, c.ps
    l = 2 * f + 1

    with nc.Block() as block:
        @block.tensor
        def _(pe):
            def batch(b):
                k = f * B + b
                pe.wait_ge(c.xt_ok, k)
                ln_tensor(c, pe, l, b, 0)
                pe.wait_ge(c.xk_ok, k + 1)
                pe.wait_ge(c.kact_ok, k)
                pe.matmul(ps[:, 2, :], c.wk[:], c.xk[:], start=True, stop=True).then_inc(c.k_ps, 1)
                pe.wait_ge(c.xr_ok, k + 1)
                pe.wait_ge(c.r_tanh, k)
                for t in range(TILES):
                    mm = pe.matmul(ps[:, 1, t * P:(t + 1) * P], c.xr[:, t * P:(t + 1) * P], c.wr[:],
                                   start=True, stop=True)
                mm.then_inc(c.r_ps, 1)
                pe.wait_ge(c.kact_ok, k + 1)
                pe.wait_ge(c.gated_ok, k)
                for t in range(TILES):
                    mm = pe.matmul(ps[:, 3, t * P:(t + 1) * P], c.k_act[:, t * P:(t + 1) * P], c.wv[:],
                                   start=True, stop=True)
                mm.then_inc(c.v_ps, 1)

            each_batch(pe, batch)

        @block.vector
        def _(dve):
            def batch(b):
                k = f * B + b
                ln_vector(c, dve, l, b)
                dve.wait_ge(c.xt_ok, k + 1)
                dve.tensor_tensor(c.dx[:], c.xt[:, 1:S + 1], c.xt[:, 0:S], ALU.subtract).then_inc(c.dx_ok, 1)
                dve.wait_ge(c.dx_ok, k + 1)
                dve.wait_ge(c.k_ps, k)
                dve.scalar_tensor_tensor(out=c.xk[:], in0=c.dx[:], scalar=c.mu[:, 1:2], in1=c.xt[:, 0:S],
                                         op0=ALU.mult, op1=ALU.add).then_inc(c.xk_ok, 1)
                dve.wait_ge(c.r_ps, k)
                dve.scalar_tensor_tensor(out=c.xr[:], in0=c.dx[:], scalar=c.mu[:, 0:1], in1=c.xt[:, 0:S],
                                         op0=ALU.mult, op1=ALU.add).then_inc(c.xr_ok, 1)
                dve.wait_ge(c.k_relu, k + 1)
                dve.wait_ge(c.v_ps, k)
                dve.scalar_tensor_tensor(out=c.k_act[:], in0=ps[:, 2, :], scalar=0.0, in1=c.relu_k[:],
                                         op0=ALU.max, op1=ALU.mult).then_inc(c.kact_ok, 1)
                dve.wait_ge(c.r_tanh, k + 1)
                dve.wait_ge(c.v_ps, k + 1)
                dve.scalar_tensor_tensor(out=c.gated[:], in0=c.tanh_r[:], scalar=1.0, in1=ps[:, 3, :],
                                         op0=ALU.add, op1=ALU.mult).then_inc(c.gated_ok, 1)
                dve.wait_ge(c.gated_ok, k + 1)
                x_b = c.x_res[:, bass.ds(b * TILES, TILES), :]
                dve.scalar_tensor_tensor(out=x_b, in0=c.gated[:].rearrange("p (t d) -> p t d", t=TILES),
                                         scalar=0.5, in1=x_b, op0=ALU.mult, op1=ALU.add).then_inc(c.f_added, 1)

            each_batch(dve, batch)

        @block.scalar
        def _(act):
            def batch(b):
                k = f * B + b
                act.wait_ge(c.ln_turned, l * B + b + 1)
                act.wait_ge(c.xr_ok, k)
                act.activation(c.xt[:, 1:S + 1], ps[:, 0, :], ACT.Copy).then_inc(c.xt_ok, 1)
                act.wait_ge(c.k_ps, k + 1)
                act.wait_ge(c.kact_ok, k)
                act.activation(c.relu_k[:], ps[:, 2, :], ACT.Relu).then_inc(c.k_relu, 1)
                act.wait_ge(c.r_ps, k + 1)
                act.wait_ge(c.gated_ok, k)
                act.activation(c.tanh_r[:], ps[:, 1, :], ACT.Tanh, scale=0.5).then_inc(c.r_tanh, 1)

            each_batch(act, batch)

        @block.gpsimd
        def _(pool):
            def batch(b):
                ln_pool(c, pool, l, b)

            each_batch(pool, batch)

        if out is not None:
            @block.sync
            def _(sp):
                def batch(b):
                    sp.wait_ge(c.f_added, f * B + b + 1)
                    sp.dma_start(out[bass.ds(b, 1), :, :].rearrange("a (t p) d -> p (a t) d", p=P),
                                 c.x_res[:, bass.ds(b * TILES, TILES), :]).then_inc(c.out_stored, 16)

                each_batch(sp, batch)
                sp.wait_ge(c.out_stored, B * 16)


def build(nc, d, out):
    with ExitStack() as ctx:
        c = Chip(nc, ctx)
        memory(c)
        semaphores(c)
        setup(c, d)
        attention_a(c)
        channel_mixing(c, 0, None)
        attention_b(c)
        channel_mixing(c, 1, out)


def kernel(**inputs):
    import numpy as np
    import concourse.bacc as bacc
    from concourse.bass_utils import run_bass_kernel_spmd

    a = {k: np.asarray(v) for k, v in inputs.items()}

    def stacked(w):
        t = w.T.reshape(P, GROUPS, BLK)
        return np.concatenate([t, t, t, np.zeros_like(t)], axis=2)

    def stacked_bias(v, fill):
        t = v.reshape(GROUPS, BLK).T
        return np.concatenate([t, t, t, np.full_like(t, fill)], axis=0)

    rows = np.arange(P)
    block, at = rows // BLK, rows % BLK
    head_mask = np.stack([np.where(block < 3, at // HD_A == j, at // 2 == j) for j in range(GROUP)], axis=1)
    causal = np.where(rows[None, :] > rows[:, None], -1e30, 0.0)
    arrays = {
        "x": a["L0_attn_a_x"],
        "wqa": stacked(a["L0_attn_a_Wq"]), "wka": stacked(a["L0_attn_a_Wk"]),
        "wva": a["L0_attn_a_Wv"].T, "woa": a["L0_attn_a_Wo"].T,
        "bqa": stacked_bias(a["L0_attn_a_bq"], 0.0), "bka": stacked_bias(a["L0_attn_a_bk"], 1.0),
        "bva": a["L0_attn_a_bv"], "boa": a["L0_attn_a_bo"],
        "wb": a["L0_attn_b_Wqkv_w"].T, "wob": a["L0_attn_b_Wo_w"].T,
        "bqkb": a["L0_attn_b_Wqkv_b"][:2 * HEADS * HD_B].reshape(2, PAIRS, P).transpose(2, 0, 1),
        "bvb": a["L0_attn_b_Wqkv_b"][2 * HEADS * HD_B:], "bob": a["L0_attn_b_Wo_b"],
        "ghost": a["L0_attn_b_ghost"],
        "wr": a["L0_ffn_W_r"].T, "wk": a["L0_ffn_W_k"].T, "wv": a["L0_ffn_W_v"].T,
        "mu": np.stack([a["L0_ffn_mu_r"], a["L0_ffn_mu_k"]], axis=1),
        "ident": np.eye(P, dtype=np.float32), "head_mask": head_mask.astype(np.float32),
        "causal": causal.astype(np.float32),
    }
    arrays = {k: np.ascontiguousarray(v) for k, v in arrays.items()}

    nc = bacc.Bacc("TRN2", target_bir_lowering=False, num_devices=1)
    d = {k: nc.dram_tensor("in_" + k, v.shape, mybir.dt.from_np(v.dtype), kind="ExternalInput").ap()
         for k, v in arrays.items()}
    out = nc.dram_tensor("out", (B, S, P), F32, kind="ExternalOutput").ap()
    build(nc, d, out)
    r = run_bass_kernel_spmd(nc, [{"in_" + k: v for k, v in arrays.items()}], core_ids=[0])
    return r.results[0]["out"]
```

```python
from contextlib import ExitStack

import concourse.bass as bass
from concourse import mybir

F32 = mybir.dt.float32
F32R = mybir.dt.float32r
BF16 = mybir.dt.bfloat16
ALU = mybir.AluOpType
ACT = mybir.ActivationFunctionType
AX_X = mybir.AxisListType.X

P = 128
B = 4
S = 512
TILES = S // P
EPS = 1e-5

HEADS = 16
HD_A = P // HEADS
GROUP = 4
GROUPS = HEADS // GROUP
BLK = GROUP * HD_A
SCALE_A = HD_A ** -0.5
M_ROWS = 3 * BLK

HD_B = 64
PAIRS = HEADS // 2
SCALE_B = HD_B ** -0.5
CAUSAL = TILES * (TILES + 1) // 2 * P
ROW_AT = [P * i * (i + 1) // 2 for i in range(TILES + 1)]
COL_AT = [sum((TILES - k) * P for k in range(n)) for n in range(TILES + 1)]
UNITS = [(0,), (1,), (2, 3)]


def nth(b, per, n):
    count = b * per + n
    return max(count, 0) if isinstance(b, int) else count


def each_batch(engine, batch):
    batch(0, False, True)
    with engine.Fori(1, B) as b:
        batch(b, True, True)
    batch(B, True, False)


class Chip:

    def __init__(self, nc, ctx):
        self.nc, self.ctx = nc, ctx

    def sb(self, name, shape, dt=F32):
        return self.ctx.enter_context(self.nc.sbuf_tensor(name, shape, dt))

    def sems(self, *names):
        return [self.ctx.enter_context(self.nc.semaphore(n)) for n in names]


def memory(c):
    c.ps = c.ctx.enter_context(c.nc.psum_tensor("ps", [P, 8, 512], F32))
    c.x_res = c.sb("x_res", [P, B * TILES, P])
    c.ident = c.sb("ident", [P, P])
    c.ident_bf = c.sb("ident_bf", [P, P], BF16)
    c.causal_bf = c.sb("causal_bf", [P, P], BF16)
    c.head_mask = c.sb("head_mask", [P, GROUP])
    c.minus_half = c.sb("minus_half", [P, TILES])
    c.eps = c.sb("eps", [P, TILES])
    c.zero = c.sb("zero", [P, 1])
    c.ln_carry = c.sb("ln_carry", [P, 1])
    c.wqa_hi = c.sb("wqa_hi", [P, GROUPS, P], F32R)
    c.wqa_lo = c.sb("wqa_lo", [P, GROUPS, P], F32R)
    c.wka_hi = c.sb("wka_hi", [P, GROUPS, P], F32R)
    c.wka_lo = c.sb("wka_lo", [P, GROUPS, P], F32R)
    c.wva_hi = c.sb("wva_hi", [P, P], F32R)
    c.wva_lo = c.sb("wva_lo", [P, P], F32R)
    c.woa = c.sb("woa", [P, P])
    c.bqa = c.sb("bqa", [P, GROUPS])
    c.bka = c.sb("bka", [P, GROUPS])
    c.bva = c.sb("bva", [P, P])
    c.boa = c.sb("boa", [P, P])
    c.wb_hi = c.sb("wb_hi", [P, 3 * HEADS * HD_B], F32R)
    c.wb_lo = c.sb("wb_lo", [P, 3 * HEADS * HD_B], F32R)
    c.wob = c.sb("wob", [P, PAIRS, P])
    c.bqkb = c.sb("bqkb", [P, 2, PAIRS])
    c.bvb = c.sb("bvb", [P, HEADS * HD_B])
    c.bob = c.sb("bob", [P, P])
    c.ghost = c.sb("ghost", [P, HEADS])
    c.wr = c.sb("wr", [P, P])
    c.wk = c.sb("wk", [P, P])
    c.wv = c.sb("wv", [P, P])
    c.mu = c.sb("mu", [P, 2])
    c.stats = c.sb("stats", [P, TILES, 6])
    c.mean_var = c.sb("mean_var", [P, TILES, 2])
    c.var_eps = c.sb("var_eps", [P, TILES])
    c.rstd = c.sb("rstd", [P, TILES])
    c.xn = c.sb("xn", [P, TILES, P])
    c.xn_hi = c.sb("xn_hi", [P, S], F32R)
    c.xn_lo = c.sb("xn_lo", [P, S], F32R)
    c.v_a = c.sb("v_a", [P, TILES, HEADS, BLK])
    c.q_stack = c.sb("q_stack", [P, GROUPS, S], F32R)
    c.k_group = c.sb("k_group", [P, S], F32R)
    c.stack = c.sb("stack", [P, 8, S], F32R)
    c.neg_max = c.sb("neg_max", [P, GROUP, TILES])
    c.max_cols = c.sb("max_cols", [P, TILES, BLK // 2, 2])
    c.probs = c.sb("probs", [P, 8, TILES * S])
    c.o_sb = c.sb("o_sb", [P, S])
    c.inv_a = c.sb("inv_a", [P, TILES, GROUP])
    c.a_tok = c.sb("a_tok", [P, TILES, P])
    c.a_chan = c.sb("a_chan", [P, S])
    c.v_b = c.sb("v_b", [P, TILES, HEADS * HD_B])
    c.neg_max_b = c.sb("neg_max_b", [P, HEADS, TILES])
    c.sum_b = c.sb("sum_b", [P, HEADS, TILES])
    c.den_b = c.sb("den_b", [P, 2, TILES])
    c.inv_b = c.sb("inv_b", [P, 2, TILES])
    c.inv_wide = c.sb("inv_wide", [P, TILES, 2, HD_B])
    c.inv_chan = c.sb("inv_chan", [P, S])


def semaphores(c):
    c.x_loaded, c.wa_loaded, c.wb_loaded, c.const_loaded, c.wf_loaded, c.out_stored = c.sems(
        "x_loaded", "wa_loaded", "wb_loaded", "const_loaded", "wf_loaded", "out_stored")
    c.w_hi, c.w_lo, c.w_bf, c.set_zero = c.sems(
        "w_hi", "w_lo", "w_bf", "set_zero")
    c.ln_stats, c.ln_mean, c.ln_eps, c.ln_rstd, c.ln_xn, c.ln_turned = c.sems(
        "ln_stats", "ln_mean", "ln_eps", "ln_rstd", "ln_xn", "ln_turned")
    c.xn_hi_ok, c.xn_lo_ok, c.x_bias = c.sems(
        "xn_hi_ok", "xn_lo_ok", "x_bias")
    c.va_ps, c.va_ok, c.ka_ps, c.ka_hi, c.ka_lo, c.km_ok = c.sems(
        "va_ps", "va_ok", "ka_ps", "ka_hi", "ka_lo", "km_ok")
    c.qa_ps, c.qa_hi, c.qa_lo, c.n_ps, c.n_max, c.m_hi = c.sems(
        "qa_ps", "qa_hi", "qa_lo", "n_ps", "n_max", "m_hi")
    c.m_lo, c.m_turned, c.m_set, c.t_ps, c.t_exp, c.oa_ps = c.sems(
        "m_lo", "m_turned", "m_set", "t_ps", "t_exp", "oa_ps")
    c.oa_sb, c.oa_turned, c.oa_inv, c.oa_tok, c.at_turned, c.at_sb = c.sems(
        "oa_sb", "oa_turned", "oa_inv", "oa_tok", "at_turned", "at_sb")
    c.woa_ps, c.a_added = c.sems(
        "woa_ps", "a_added")
    c.vb_ps, c.vb_ok, c.qb_ps, c.qb_hi, c.qb_lo, c.kb_ps = c.sems(
        "vb_ps", "vb_ok", "qb_ps", "qb_hi", "qb_lo", "kb_ps")
    c.kb_hi, c.kb_lo, c.s_ps, c.s_max, c.s_exp, c.xp_ps = c.sems(
        "kb_hi", "kb_lo", "s_ps", "s_max", "s_exp", "xp_ps")
    c.xp_act, c.xp_dve, c.den_ok, c.inv_ok, c.wide_ok, c.inv_turned = c.sems(
        "xp_act", "xp_dve", "den_ok", "inv_ok", "wide_ok", "inv_turned")
    c.inv_sb, c.ob_ps, c.ob_sb, c.wob_ps, c.b_added = c.sems(
        "inv_sb", "ob_ps", "ob_sb", "wob_ps", "b_added")
    (c.xt_zero,) = c.sems("xt_zero")
    c.xt_ok, c.dx_ok, c.xr_ok, c.xk_ok, c.r_ps, c.k_ps = c.sems(
        "xt_ok", "dx_ok", "xr_ok", "xk_ok", "r_ps", "k_ps")
    c.r_tanh, c.k_relu, c.kact_ok, c.v_ps, c.gated_ok, c.f_added = c.sems(
        "r_tanh", "k_relu", "kact_ok", "v_ps", "gated_ok", "f_added")


def setup(c, d):
    nc = c.nc
    raw = c.probs[:].rearrange("p s n -> p (s n)")
    n_b = 3 * HEADS * HD_B
    raw_qa = raw[:, n_b:n_b + 512].rearrange("p (g n) -> p g n", g=GROUPS)
    raw_ka = raw[:, n_b + 512:n_b + 1024].rearrange("p (g n) -> p g n", g=GROUPS)
    raw_va = raw[:, n_b + 1024:n_b + 1152]
    raw_causal = raw[:, n_b + 1152:n_b + 1280]
    with nc.Block() as block:
        @block.sync
        def _(sp):
            for b in range(B):
                sp.dma_start(c.x_res[:, b * TILES:(b + 1) * TILES, :],
                             d["x"][b].rearrange("(t p) d -> p t d", p=P)).then_inc(c.x_loaded, 16)
            for dst, src in ((c.woa[:], d["woa"]), (c.bva[:], d["bva"].partition_broadcast(P)),
                             (c.boa[:], d["boa"].partition_broadcast(P)), (c.bqa[:], d["bqa"]),
                             (c.bka[:], d["bka"]), (c.wr[:], d["wr"]), (c.wk[:], d["wk"]), (c.wv[:], d["wv"]),
                             (c.mu[:], d["mu"]), (c.ghost[:], d["ghost"].partition_broadcast(P)),
                             (c.bob[:], d["bob"].partition_broadcast(P)),
                             (c.bvb[:], d["bvb"].partition_broadcast(P)), (c.bqkb[:], d["bqkb"]),
                             (c.wob[:], d["wob"].rearrange("(h p) d -> p h d", p=P))):
                sp.dma_start(dst, src).then_inc(c.wf_loaded, 16)
            sp.wait_ge(c.x_loaded, B * 16)
            sp.wait_ge(c.wf_loaded, 14 * 16)

        @block.scalar
        def _(act):
            act.dma_start(raw_qa, d["wqa"]).then_inc(c.wa_loaded, 16)
            act.dma_start(raw_ka, d["wka"]).then_inc(c.wa_loaded, 16)
            act.dma_start(raw_va, d["wva"]).then_inc(c.wa_loaded, 16)
            act.dma_start(raw[:, 0:n_b], d["wb"]).then_inc(c.wb_loaded, 16)
            for dst, src in ((c.ident[:], d["ident"]), (c.head_mask[:], d["head_mask"]),
                             (raw_causal, d["causal"])):
                act.dma_start(dst, src).then_inc(c.const_loaded, 16)
            act.wait_ge(c.const_loaded, 48)

        @block.vector
        def _(dve):
            dve.memset(c.v_a[:], 0.0).then_inc(c.set_zero, 1)
            dve.memset(c.max_cols[:], 0.0).then_inc(c.set_zero, 1)
            dve.memset(c.minus_half[:], -0.5).then_inc(c.set_zero, 1)
            dve.memset(c.eps[:], EPS).then_inc(c.set_zero, 1)
            dve.memset(c.zero[:], 0.0).then_inc(c.set_zero, 1)
            dve.wait_ge(c.set_zero, 1)
            dve.memset(c.v_a[:, :, :, HD_A:HD_A + 1], 1.0).then_inc(c.set_zero, 1)
            dve.wait_ge(c.wa_loaded, 48)
            n = 0
            for hi, lo, w in ((c.wqa_hi[:], c.wqa_lo[:], raw_qa), (c.wka_hi[:], c.wka_lo[:], raw_ka),
                              (c.wva_hi[:], c.wva_lo[:], raw_va)):
                dve.tensor_copy(hi, w).then_inc(c.w_hi, 1)
                n += 1
                dve.wait_ge(c.w_hi, n)
                dve.tensor_tensor(lo, w, hi.bitcast(F32), ALU.subtract).then_inc(c.w_lo, 1)
            dve.wait_ge(c.const_loaded, 48)
            dve.tensor_copy(c.ident_bf[:], c.ident[:]).then_inc(c.w_bf, 1)
            dve.tensor_copy(c.causal_bf[:], raw_causal).then_inc(c.w_bf, 1)
            dve.wait_ge(c.wb_loaded, 16)
            for at in range(0, n_b, 1024):
                w = raw[:, at:at + 1024]
                scale = SCALE_B if at == 0 else 1.0
                dve.tensor_scalar(c.wb_hi[:, at:at + 1024], w, scale, None, ALU.mult).then_inc(c.w_hi, 1)
                n += 1
                dve.wait_ge(c.w_hi, n)
                dve.scalar_tensor_tensor(out=c.wb_lo[:, at:at + 1024], in0=w, scalar=scale,
                                         in1=c.wb_hi[:, at:at + 1024].bitcast(F32),
                                         op0=ALU.mult, op1=ALU.subtract).then_inc(c.w_lo, 1)
            dve.wait_ge(c.w_lo, 6)
            dve.wait_ge(c.wf_loaded, 14 * 16)
            dve.tensor_scalar(c.bqkb[:, 0, :], c.bqkb[:, 0, :], SCALE_B, None, ALU.mult).then_inc(c.w_hi, 1)


def ln_statistics(c, dve, l, b):
    k = l * B + b
    for t in range(TILES):
        dve.bn_stats(c.stats[:, t, :], c.x_res[:, bass.ds(b * TILES + t, 1), :]
                     .rearrange("p a d -> p (a d)")).then_inc(c.ln_stats, 1)
    dve.wait_ge(c.ln_eps, k)
    dve.wait_ge(c.ln_stats, nth(k, TILES, TILES))
    dve.memset(c.ln_carry[:], 0.0)
    for t in range(TILES):
        dve.bn_aggr(c.mean_var[:, t, :], c.stats[:, t, :]).then_inc(c.ln_mean, 1)


def ln_normalise(c, dve, l, b):
    k = l * B + b
    dve.wait_ge(c.ln_rstd, k + 1)
    dve.wait_ge(c.ln_turned, k)
    for t in range(TILES):
        dve.tensor_scalar(c.xn[:, t, :], c.x_res[:, bass.ds(b * TILES + t, 1), :]
                          .rearrange("p a d -> p (a d)"), c.mean_var[:, t, 0:1], c.rstd[:, t:t + 1],
                          ALU.subtract, ALU.mult).then_inc(c.ln_xn, 1)


def ln_pool(c, pool, l, b):
    k = l * B + b
    pool.wait_ge(c.ln_mean, nth(k, TILES, TILES))
    pool.tensor_tensor(c.var_eps[:], c.mean_var[:, :, 1], c.eps[:], ALU.add).then_inc(c.ln_eps, 1)
    pool.wait_ge(c.ln_eps, k + 1)
    pool.wait_ge(c.ln_xn, nth(k, TILES, 0))
    pool.tensor_tensor(c.rstd[:], c.var_eps[:], c.minus_half[:], ALU.pow).then_inc(c.ln_rstd, 1)


def ln_tensor(c, pe, l, b, bank):
    k = l * B + b
    for t in range(TILES):
        pe.wait_ge(c.ln_xn, nth(k, TILES, t + 1))
        mm = pe.transpose(c.ps[:, bank, t * P:(t + 1) * P], c.xn[:, t, :], c.ident[:])
    mm.then_inc(c.ln_turned, 1)


def three_passes(pe, out, lhs, rhs):
    (lh, ll), (rh, rl) = lhs, rhs
    pe.matmul(out, lh, rh, start=True, stop=False)
    pe.matmul(out, ll, rh, start=False, stop=False)
    return pe.matmul(out, lh, rl, start=False, stop=True)


def add_bias(c, pool, l, b, bias):
    pool.wait_ge(c.ln_xn, nth(l * B + b, TILES, TILES))
    x_b = c.x_res[:, bass.ds(b * TILES, TILES), :]
    pool.tensor_tensor(x_b, x_b, bias[:].rearrange("p (a d) -> p a d", a=1).broadcast_to([P, TILES, P]),
                       ALU.add).then_inc(c.x_bias, 1)


def attention_a(c):
    nc, ps = c.nc, c.ps
    MAXIMA = HEADS * TILES
    HALVES = HEADS * 2

    def k_stack(g, j):
        return c.stack[:, GROUP * (g % 2) + j, :]

    def q_stack(g):
        return c.q_stack[:, g % GROUPS, :]

    def probs(g, j):
        return c.probs[:, GROUP * (g % 2) + j, :]

    with nc.Block() as block:
        @block.tensor
        def _(pe):
            def project_k(b, g):
                three_passes(pe, ps[:, 7, :], (c.wka_hi[:, g, :], c.wka_lo[:, g, :]), (c.xn_hi[:], c.xn_lo[:]))\
                    .then_inc(c.ka_ps, 1)

            def project_q(b, g):
                pe.wait_ge(c.ka_lo, nth(b, GROUPS, g + 1))
                three_passes(pe, ps[:, 7, :], (c.wqa_hi[:, g, :], c.wqa_lo[:, g, :]), (c.xn_hi[:], c.xn_lo[:]))\
                    .then_inc(c.qa_ps, 1)

            def project_values(b):
                pe.wait_ge(c.oa_sb, nth(b, GROUPS, 0))
                for t in range(TILES):
                    tok = slice(t * P, (t + 1) * P)
                    mm = three_passes(pe, ps[:, 6, tok], (c.xn_hi[:, tok], c.xn_lo[:, tok]),
                                      (c.wva_hi[:], c.wva_lo[:]))
                mm.then_inc(c.va_ps, 1)

            def scores(b, g, i):
                j, qt = divmod(i, TILES)
                n = 16 * g + i
                if i == 0:
                    pe.wait_ge(c.qa_lo, nth(b, GROUPS, g + 1))
                if qt == 0:
                    pe.wait_ge(c.km_ok, nth(b, HEADS, GROUP * g + j + 1))
                pe.wait_ge(c.n_max, nth(b, MAXIMA, n - 1))
                pe.matmul(ps[:, n % 2, :], q_stack(g)[:, qt * P:(qt + 1) * P], k_stack(g, j),
                          start=True, stop=True).then_inc(c.n_ps, 1)

            def turn_maxima(b, g):
                pe.wait_ge(c.m_lo, nth(b, GROUPS, g + 1))
                for qt in range(TILES):
                    mm = pe.transpose(ps[0:BLK, 7, qt * P:(qt + 1) * P],
                                      c.max_cols[:, qt, :, :].rearrange("p a b -> p (a b)"), c.ident[:])
                mm.then_inc(c.m_turned, 1)

            def scores_turned(b, g, i):
                j, kt = divmod(i, TILES)
                half = 8 * g + 2 * j + kt // 2
                if i == 0:
                    pe.wait_ge(c.m_set, nth(b, GROUPS, g + 1))
                if kt % 2 == 0:
                    pe.wait_ge(c.t_exp, nth(b, HALVES, half - 1))
                mm = pe.matmul(ps[:, 2 + 2 * (half % 2) + kt % 2, :], k_stack(g, j)[:, kt * P:(kt + 1) * P],
                               q_stack(g), start=True, stop=True)
                if kt % 2 == 1:
                    mm.then_inc(c.t_ps, 1)

            def times_values(b, g, kt):
                if kt == 0:
                    pe.wait_ge(c.va_ok, nth(b, 1, 1 if g >= 0 else 0))
                    pe.wait_ge(c.t_exp, nth(b, HALVES, 8 * g + 8))
                    pe.wait_ge(c.oa_sb, nth(b, GROUPS, g))
                    if g == 0:
                        pe.wait_ge(c.a_added, nth(b, 1, 0))
                for j in range(GROUP):
                    mm = pe.matmul(ps[BLK * j:BLK * (j + 1), 6, :], c.v_a[:, kt, (GROUP * g + j) % HEADS, :],
                                   probs(g, j)[:, kt * S:(kt + 1) * S], start=(kt == 0), stop=(kt == TILES - 1))
                if kt == TILES - 1:
                    mm.then_inc(c.oa_ps, 1)

            def turn_output(b, g):
                pe.wait_ge(c.oa_sb, nth(b, GROUPS, g + 1))
                for qt in range(TILES):
                    mm = pe.transpose(ps[:, 7, qt * P:(qt + 1) * P], c.o_sb[:, qt * P:(qt + 1) * P], c.ident[:])
                mm.then_inc(c.oa_turned, 1)

            def turn_batch(b):
                pe.wait_ge(c.oa_tok, nth(b, GROUPS, 0))
                for t in range(TILES):
                    mm = pe.transpose(ps[:, 6, t * P:(t + 1) * P], c.a_tok[:, t, :], c.ident[:])
                mm.then_inc(c.at_turned, 1)

            def output_product(b):
                pe.wait_ge(c.at_sb, nth(b, 1, 0))
                for t in range(TILES):
                    mm = pe.matmul(ps[:, 6, t * P:(t + 1) * P], c.a_chan[:, t * P:(t + 1) * P], c.woa[:],
                                   start=True, stop=True)
                mm.then_inc(c.woa_ps, 1)

            def batch(b, prev, own):
                for i in range(16):
                    if prev and i == 0:
                        pe.wait_ge(c.oa_tok, nth(b, GROUPS, -3))
                        turn_maxima(b, -1)
                    if prev:
                        scores_turned(b, -1, i)
                    if prev and i == 2:
                        pe.wait_ge(c.m_set, nth(b, GROUPS, 0))
                        turn_output(b, -3)
                    if prev and i % 4 == 3:
                        times_values(b, -2, i // 4)
                    if own and i == 5:
                        pe.wait_ge(c.oa_tok, nth(b, GROUPS, -2))
                        ln_tensor(c, pe, 0, b, 7)
                    if own and i == 11:
                        pe.wait_ge(c.xn_lo_ok, b + 1)
                        project_k(b, 0)
                if own:
                    project_q(b, 0)
                for i in range(16):
                    if own:
                        scores(b, 0, i)
                    if prev and i % 4 == 3:
                        times_values(b, -1, i // 4)
                    if prev and i == 4:
                        if own:
                            pe.wait_ge(c.qa_lo, nth(b, GROUPS, 1))
                        else:
                            pe.wait_ge(c.oa_tok, nth(b, GROUPS, -2))
                        turn_output(b, -2)
                    if own and i == 6:
                        pe.wait_ge(c.oa_tok, nth(b, GROUPS, -1))
                        pe.wait_ge(c.qa_lo, nth(b, GROUPS, 1))
                        project_k(b, 1)
                    if own and i == 10:
                        project_q(b, 1)
                for i in range(16 + 3):
                    if own and i < 16:
                        scores(b, 1, i)
                    if own and i == 1:
                        pe.wait_ge(c.qa_lo, nth(b, GROUPS, 2))
                        turn_maxima(b, 0)
                    if own and i >= 3:
                        scores_turned(b, 0, i - 3)
                    if prev and i == 4:
                        if own:
                            pe.wait_ge(c.m_set, nth(b, GROUPS, 1))
                        pe.wait_ge(c.oa_tok, nth(b, GROUPS, -1))
                        turn_output(b, -1)
                    if own and i == 5:
                        project_values(b)
                    if own and i == 7:
                        pe.wait_ge(c.oa_tok, nth(b, GROUPS, 0))
                        pe.wait_ge(c.m_set, nth(b, GROUPS, 1))
                        project_k(b, 2)
                    if own and i == 10:
                        project_q(b, 2)
                    if prev and i == 12:
                        if own:
                            pe.wait_ge(c.va_ok, nth(b, 1, 1))
                        else:
                            pe.wait_ge(c.oa_sb, nth(b, GROUPS, 0))
                        turn_batch(b)
                    if prev and i == 18:
                        output_product(b)
                if not own:
                    return
                for i in range(16 + 3):
                    if i < 16:
                        scores(b, 2, i)
                    if i == 1:
                        pe.wait_ge(c.qa_lo, nth(b, GROUPS, 3))
                        turn_maxima(b, 1)
                    if i >= 3:
                        scores_turned(b, 1, i - 3)
                    if i == 6:
                        pe.wait_ge(c.m_set, nth(b, GROUPS, 2))
                        project_k(b, 3)
                    if i == 10:
                        project_q(b, 3)
                    if i % 4 == 2 and i < 16:
                        times_values(b, 0, i // 4)
                for i in range(16 + 3):
                    if i < 16:
                        scores(b, 3, i)
                    if i == 1:
                        pe.wait_ge(c.qa_lo, nth(b, GROUPS, 4))
                        turn_maxima(b, 2)
                    if i >= 3:
                        scores_turned(b, 2, i - 3)
                    if i == 5:
                        pe.wait_ge(c.m_set, nth(b, GROUPS, 3))
                        turn_output(b, 0)
                    if i % 4 == 2 and i < 16:
                        times_values(b, 1, i // 4)

            each_batch(pe, batch)

        @block.vector
        def _(dve):
            def k_low(b, g):
                rows = slice(BLK, 2 * BLK)
                dve.wait_ge(c.ka_hi, nth(b, GROUPS, g + 1))
                dve.scalar_tensor_tensor(out=c.k_group[rows, :], in0=ps[rows, 7, :], scalar=c.bka[rows, g:g + 1],
                                         in1=c.k_group[rows, :].bitcast(F32), op0=ALU.add, op1=ALU.subtract)\
                   .then_inc(c.ka_lo, 1)

            def q_low(b, g):
                rows = slice(2 * BLK, 3 * BLK)
                dve.wait_ge(c.qa_hi, nth(b, GROUPS, g + 1))
                dve.scalar_tensor_tensor(out=q_stack(g)[rows, :], in0=ps[rows, 7, :],
                                         scalar=c.bqa[rows, g:g + 1], in1=q_stack(g)[rows, :].bitcast(F32),
                                         op0=ALU.add, op1=ALU.subtract).then_inc(c.qa_lo, 1)

            def mask_keys(b, g, j):
                if j == 0:
                    dve.wait_ge(c.ka_lo, nth(b, GROUPS, g + 1))
                dve.wait_ge(c.t_ps, nth(b, HALVES, 8 * (g - 2) + 2 * j + 2))
                dve.tensor_scalar(k_stack(g, j), c.k_group[:].bitcast(F32), c.head_mask[:, j:j + 1], None,
                                  ALU.mult).then_inc(c.km_ok, 1)

            def maximum(b, g, i):
                j, qt = divmod(i, TILES)
                n = 16 * g + i
                dve.wait_ge(c.n_ps, nth(b, MAXIMA, n + 1))
                if i == 0:
                    dve.wait_ge(c.m_lo, nth(b, GROUPS, g))
                dve.tensor_reduce(c.neg_max[:, j, qt:qt + 1], ps[:, n % 2, :], AX_X, ALU.max, negate=True)\
                   .then_inc(c.n_max, 1)

            def split_maxima(b, g):
                nm = c.neg_max[:].rearrange("p j t -> p t j")
                dve.wait_ge(c.n_max, nth(b, MAXIMA, 16 * g + 16))
                dve.wait_ge(c.m_turned, nth(b, GROUPS, g))
                dve.tensor_copy(c.max_cols[:, :, 0:GROUP, 0].bitcast(F32R), nm).then_inc(c.m_hi, 1)
                dve.wait_ge(c.m_hi, nth(b, GROUPS, g + 1))
                dve.tensor_tensor(c.max_cols[:, :, 0:GROUP, 1], nm, c.max_cols[:, :, 0:GROUP, 0],
                                  ALU.subtract).then_inc(c.m_lo, 1)

            def divide(b, g):
                at = BLK * (g % GROUPS)
                o = ps[:, 7, :].rearrange("p (t j d) -> p t j d", t=TILES, j=GROUP)
                dve.wait_ge(c.oa_turned, nth(b, GROUPS, g + 1))
                dve.reciprocal(c.inv_a[:], o[:, :, :, HD_A]).then_inc(c.oa_inv, 1)
                dve.wait_ge(c.oa_inv, nth(b, GROUPS, g + 1))
                if g == 0:
                    dve.wait_ge(c.at_turned, nth(b, 1, 0))
                dve.tensor_tensor(c.a_tok[:, :, at:at + BLK].rearrange("p t (j d) -> p t j d", j=GROUP),
                                  o[:, :, :, 0:HD_A],
                                  c.inv_a[:].rearrange("p t (j a) -> p t j a", a=1)
                                  .broadcast_to([P, TILES, GROUP, HD_A]), ALU.mult).then_inc(c.oa_tok, 1)

            def keep_values(b):
                dve.wait_ge(c.va_ps, nth(b, 1, 1))
                dve.wait_ge(c.oa_ps, nth(b, GROUPS, 0))
                dve.tensor_tensor(c.v_a[:, :, :, 0:HD_A],
                                  ps[:, 6, :].rearrange("p (t h d) -> p t h d", t=TILES, h=HEADS),
                                  c.bva[:].rearrange("p (a h d) -> p a h d", a=1, h=HEADS)
                                  .broadcast_to([P, TILES, HEADS, HD_A]), ALU.add).then_inc(c.va_ok, 1)

            def add_output(b):
                dve.wait_ge(c.woa_ps, nth(b, 1, 0))
                dve.wait_ge(c.x_bias, nth(b, 1, 0))
                x_b = c.x_res[:, bass.ds((b - 1) * TILES, TILES), :]
                dve.tensor_tensor(x_b, ps[:, 6, :].rearrange("p (t d) -> p t d", t=TILES), x_b, ALU.add)\
                   .then_inc(c.a_added, 1)

            def batch(b, prev, own):
                if own:
                    ln_statistics(c, dve, 0, b)
                    ln_normalise(c, dve, 0, b)
                if prev:
                    divide(b, -3)
                if own:
                    dve.wait_ge(c.xn_hi_ok, b + 1)
                    dve.tensor_tensor(c.xn_lo[:], ps[:, 7, :], c.xn_hi[:].bitcast(F32), ALU.subtract)\
                       .then_inc(c.xn_lo_ok, 1)
                    k_low(b, 0)
                    mask_keys(b, 0, 0)
                    q_low(b, 0)
                    for j in range(1, GROUP):
                        mask_keys(b, 0, j)
                if not own:
                    divide(b, -2)
                    divide(b, -1)
                    add_output(b)
                    return
                for s in range(GROUPS):
                    for i in range(16):
                        maximum(b, s, i)
                        if i == 5 and s == 0 and prev:
                            divide(b, -2)
                        if i == 5 and s == 1 and prev:
                            divide(b, -1)
                        if i == 7 and s == 1:
                            keep_values(b)
                        if i == 7 and s == 3:
                            divide(b, 0)
                        if i == 9 and s + 1 < GROUPS:
                            k_low(b, s + 1)
                    if s + 1 < GROUPS:
                        q_low(b, s + 1)
                        mask_keys(b, s + 1, 0)
                    split_maxima(b, s)
                    if s + 1 < GROUPS:
                        for j in range(1, GROUP):
                            mask_keys(b, s + 1, j)
                    if s == 1 and prev:
                        add_output(b)

            each_batch(dve, batch)

        @block.scalar
        def _(act):
            def k_high(b, g):
                act.wait_ge(c.ka_ps, nth(b, GROUPS, g + 1))
                act.wait_ge(c.km_ok, nth(b, HEADS, GROUP * g))
                act.activation(c.k_group[:], ps[:, 7, :], ACT.Identity, bias=c.bka[:, g:g + 1])\
                   .then_inc(c.ka_hi, 1)

            def q_high(b, g):
                act.wait_ge(c.qa_ps, nth(b, GROUPS, g + 1))
                act.wait_ge(c.t_ps, nth(b, HALVES, 8 * (g - GROUPS) + 8))
                act.activation(q_stack(g), ps[:, 7, :], ACT.Identity, bias=c.bqa[:, g:g + 1])\
                   .then_inc(c.qa_hi, 1)

            def set_maxima(b, g):
                act.wait_ge(c.m_turned, nth(b, GROUPS, g + 1))
                act.activation(c.q_stack[M_ROWS:P, g % GROUPS, :], ps[0:BLK, 7, :], ACT.Copy).then_inc(c.m_set, 1)

            def exponentials(b, g, n):
                half = 8 * g + n
                act.wait_ge(c.t_ps, nth(b, HALVES, half + 1))
                if n == 0:
                    act.wait_ge(c.oa_ps, nth(b, GROUPS, g - 1))
                at = 2 + 2 * (half % 2)
                col = 2 * (n % 2) * S
                act.activation(probs(g, n // 2)[:, col:col + 2 * S].rearrange("p (k n) -> p k n", k=2),
                               ps[:, at:at + 2, :], ACT.Exp, scale=SCALE_A).then_inc(c.t_exp, 1)

            def keep_output(b, g):
                act.wait_ge(c.oa_ps, nth(b, GROUPS, g + 1))
                act.wait_ge(c.oa_turned, nth(b, GROUPS, g))
                act.activation(c.o_sb[:], ps[:, 6, :], ACT.Copy).then_inc(c.oa_sb, 1)

            def keep_turned(b):
                act.wait_ge(c.at_turned, nth(b, 1, 0))
                act.wait_ge(c.woa_ps, nth(b, 1, -1))
                act.activation(c.a_chan[:], ps[:, 6, :], ACT.Copy).then_inc(c.at_sb, 1)

            def batch(b, prev, own):
                if prev:
                    set_maxima(b, -1)
                for n in range(8):
                    if own and n == 4:
                        act.wait_ge(c.ln_turned, b + 1)
                        act.wait_ge(c.qa_ps, nth(b, GROUPS, 0))
                        act.wait_ge(c.va_ps, nth(b, 1, 0))
                        act.activation(c.xn_hi[:], ps[:, 7, :], ACT.Copy).then_inc(c.xn_hi_ok, 1)
                    if own and n == 6:
                        k_high(b, 0)
                    if own and n == 7:
                        q_high(b, 0)
                    if prev:
                        exponentials(b, -1, n)
                if prev:
                    keep_output(b, -2)
                if own:
                    k_high(b, 1)
                    q_high(b, 1)
                if prev:
                    keep_output(b, -1)
                if not own:
                    keep_turned(b)
                    return
                for s in range(1, GROUPS):
                    set_maxima(b, s - 1)
                    for n in range(8):
                        exponentials(b, s - 1, n)
                        if n == 1 and s + 1 < GROUPS:
                            k_high(b, s + 1)
                        if n == 3 and s + 1 < GROUPS:
                            q_high(b, s + 1)
                        if n == 5 and s == 1 and prev:
                            keep_turned(b)
                    if s >= 2:
                        keep_output(b, s - 2)

            each_batch(act, batch)

        @block.gpsimd
        def _(pool):
            def batch(b, prev, own):
                if own:
                    ln_pool(c, pool, 0, b)
                    add_bias(c, pool, 0, b, c.boa)

            each_batch(pool, batch)


def attention_b(c):
    nc, ps = c.nc, c.ps
    SCORES = PAIRS * TILES
    flat = c.probs[:].rearrange("p s n -> p (s n)")

    def part(p, which):
        return c.stack[:, 4 * (p % 2) + which, :]

    def p_at(p, a):
        at = (2 * (p % 2) + a) * CAUSAL
        return flat[:, at:at + CAUSAL]

    def pt_at(p, a):
        at = (4 + 2 * (p % 2) + a) * CAUSAL
        return flat[:, at:at + CAUSAL]

    def out_at(p):
        at = 8 * CAUSAL + (p % PAIRS) * S
        return flat[:, at:at + S]

    def unit_columns(u):
        return COL_AT[UNITS[u][0]], sum(TILES - k for k in UNITS[u]) * P

    def unit_bank(a, u):
        return 4 + (3 * a + u) % 2

    def values_before(p):
        return 2 * TILES if p >= 0 else 0

    with nc.Block() as block:
        @block.tensor
        def _(pe):
            def project(p, which, bank, done):
                col = which * HEADS * HD_B + p * P
                three_passes(pe, ps[:, bank, :], (c.wb_hi[:, col:col + P], c.wb_lo[:, col:col + P]),
                             (c.xn_hi[:], c.xn_lo[:])).then_inc(done, 1)

            def scores(b, p, i):
                w = (i + 1) * P
                q = slice(i * P, (i + 1) * P)
                if i == 0:
                    pe.wait_ge(c.qb_lo, nth(b, PAIRS, p + 1))
                    pe.wait_ge(c.kb_lo, nth(b, PAIRS, p + 1))
                pe.wait_ge(c.s_exp, nth(b, 2 * SCORES, 8 * p + 2 * i - 2))
                for q_part, k_part in ((0, 2), (1, 2), (0, 3)):
                    for a in range(2):
                        rows = slice(HD_B * a, HD_B * (a + 1))
                        pe.matmul(ps[:, 2 * (i % 2) + a, 0:w], part(p, q_part)[rows, q], part(p, k_part)[rows, 0:w],
                                  start=(q_part, k_part) == (0, 2), stop=False)
                for a in range(2):
                    mm = pe.matmul(ps[:, 2 * (i % 2) + a, i * P:w], c.ident_bf[:], c.causal_bf[:],
                                   start=False, stop=True)
                mm.then_inc(c.s_ps, 1)

            def turn(b, p, a, u):
                if u == 0:
                    pe.wait_ge(c.s_exp, nth(b, 2 * SCORES, 8 * p + 7 + a))
                if p == 0 and a == 0 and u < 2:
                    pe.wait_ge(c.vb_ok, nth(b, 2 * TILES, 2 * TILES - 1 + u))
                if (a, u) in ((0, 2), (1, 2)):
                    pe.wait_ge(c.xp_act, nth(b, HEADS, 2 * p + a + 1))
                elif a == 0:
                    pe.wait_ge(c.xp_dve, nth(b, 2 * HEADS, 4 * (p - 1) + 3 + u))
                else:
                    pe.wait_ge(c.xp_dve, nth(b, 2 * HEADS, 4 * p + 1 + u))
                col = 0
                for kt in UNITS[u]:
                    for qt in range(kt, TILES):
                        at = ROW_AT[qt] + kt * P
                        mm = pe.transpose(ps[:, unit_bank(a, u), col:col + P], p_at(p, a)[:, at:at + P], c.ident[:])
                        col += P
                mm.then_inc(c.xp_ps, 1)

            def turn_reciprocals(b, p):
                pe.wait_ge(c.inv_sb, nth(b, PAIRS, p))
                pe.wait_ge(c.wide_ok, nth(b, PAIRS, p + 1))
                for qt in range(TILES):
                    mm = pe.transpose(ps[:, 7, qt * P:(qt + 1) * P],
                                      c.inv_wide[:, qt, :, :].rearrange("p a d -> p (a d)"), c.ident[:])
                mm.then_inc(c.inv_turned, 1)

            def times_values(b, p, kt):
                if kt == 0:
                    pe.wait_ge(c.vb_ok, nth(b, 2 * TILES, values_before(p)))
                    pe.wait_ge(c.ob_sb, nth(b, PAIRS, p))
                    if p == 0:
                        pe.wait_ge(c.b_added, nth(b, 1, 0))
                    pe.wait_ge(c.xp_act, nth(b, HEADS, 2 * p + 2))
                    pe.wait_ge(c.xp_dve, nth(b, 2 * HEADS, 4 * p + 4))
                w = (TILES - kt) * P
                for a in range(2):
                    h = (2 * p + a) % HEADS
                    mm = pe.matmul(ps[HD_B * a:HD_B * (a + 1), 6, kt * P:S], c.v_b[:, kt, h * HD_B:(h + 1) * HD_B],
                                   pt_at(p, a)[:, COL_AT[kt]:COL_AT[kt] + w],
                                   start=(kt == 0), stop=(kt == TILES - 1))
                if kt == TILES - 1:
                    mm.then_inc(c.ob_ps, 1)

            def project_values(b, n):
                t, half = divmod(n, 2)
                tok = slice(t * P, (t + 1) * P)
                col = 2 * HEADS * HD_B + half * S
                if n < 2:
                    pe.wait_ge(c.xp_dve, nth(b, 2 * HEADS, n - 1))
                else:
                    pe.wait_ge(c.vb_ok, nth(b, 2 * TILES, n - 1))
                three_passes(pe, ps[:, 4 + n % 2, :], (c.xn_hi[:, tok], c.xn_lo[:, tok]),
                             (c.wb_hi[:, col:col + S], c.wb_lo[:, col:col + S])).then_inc(c.vb_ps, 1)

            def output_product(b, t):
                if t == 0:
                    pe.wait_ge(c.ob_sb, nth(b, PAIRS, 0))
                for p in range(PAIRS):
                    mm = pe.matmul(ps[:, 6, t * P:(t + 1) * P], out_at(p)[:, t * P:(t + 1) * P],
                                   c.wob[:, p, :], start=(p == 0), stop=(p == PAIRS - 1))
                if t == TILES - 1:
                    mm.then_inc(c.wob_ps, 1)

            def batch(b, prev, own):
                if prev:
                    turn(b, -1, 0, 0)
                    turn(b, -1, 0, 1)
                    turn_reciprocals(b, -2)
                if own:
                    pe.wait_ge(c.s_exp, nth(b, 2 * SCORES, -1))
                    ln_tensor(c, pe, 2, b, 2)
                if prev:
                    times_values(b, -2, 0)
                    turn(b, -1, 0, 2)
                    turn(b, -1, 1, 0)
                    times_values(b, -2, 1)
                if own:
                    pe.wait_ge(c.xn_lo_ok, B + b + 1)
                    pe.wait_ge(c.s_exp, nth(b, 2 * SCORES, 0))
                    project(0, 0, 0, c.qb_ps)
                if prev:
                    turn(b, -1, 1, 1)
                    times_values(b, -2, 2)
                    times_values(b, -2, 3)
                    turn(b, -1, 1, 2)
                if own:
                    project(0, 1, 1, c.kb_ps)
                if prev:
                    times_values(b, -1, 0)
                    times_values(b, -1, 1)
                    turn_reciprocals(b, -1)
                    times_values(b, -1, 2)
                    times_values(b, -1, 3)
                if prev and not own:
                    for t in range(TILES):
                        output_product(b, t)
                if not own:
                    return
                for p in range(PAIRS):
                    scores(b, p, 0)
                    if p + 1 < PAIRS:
                        pe.wait_ge(c.inv_sb, nth(b, PAIRS, max(p - 2, 0)))
                        pe.wait_ge(c.kb_lo, nth(b, PAIRS, p + 1))
                        project(p + 1, 0, 7, c.qb_ps)
                    if p == 0:
                        project_values(b, 0)
                        project_values(b, 1)
                    else:
                        turn(b, p - 1, 0, 0)
                        turn(b, p - 1, 0, 1)
                    scores(b, p, 1)
                    if p + 1 < PAIRS:
                        pe.wait_ge(c.qb_lo, nth(b, PAIRS, p + 2))
                        project(p + 1, 1, 7, c.kb_ps)
                    if p == 0:
                        project_values(b, 2)
                        project_values(b, 3)
                    else:
                        turn(b, p - 1, 0, 2)
                    if p >= 2:
                        times_values(b, p - 2, 0)
                    elif prev:
                        output_product(b, 2 * p)
                    scores(b, p, 2)
                    if p == 0:
                        project_values(b, 4)
                        project_values(b, 5)
                    else:
                        turn(b, p - 1, 1, 0)
                        turn(b, p - 1, 1, 1)
                    if p >= 2:
                        times_values(b, p - 2, 1)
                    elif prev:
                        output_product(b, 2 * p + 1)
                    scores(b, p, 3)
                    if p >= 2:
                        pe.wait_ge(c.kb_lo, nth(b, PAIRS, min(p + 2, PAIRS)))
                        turn_reciprocals(b, p - 2)
                    if p == 0:
                        project_values(b, 6)
                        project_values(b, 7)
                    else:
                        turn(b, p - 1, 1, 2)
                    if p >= 2:
                        times_values(b, p - 2, 2)
                        times_values(b, p - 2, 3)

            each_batch(pe, batch)

        @block.vector
        def _(dve):
            def low(b, p, which, bank, hi_ready, done):
                dve.wait_ge(hi_ready, nth(b, PAIRS, p + 1))
                dve.scalar_tensor_tensor(out=part(p, 2 * which + 1), in0=ps[:, bank, :],
                                         scalar=c.bqkb[:, which, p:p + 1], in1=part(p, 2 * which).bitcast(F32),
                                         op0=ALU.add, op1=ALU.subtract).then_inc(done, 1)

            def maxima(b, p, i):
                n = TILES * p + i
                at = 2 * (i % 2)
                dve.wait_ge(c.s_ps, nth(b, SCORES, n + 1))
                if n == 0:
                    dve.wait_ge(c.s_exp, nth(b, 2 * SCORES, 0))
                dve.tensor_reduce(c.neg_max_b[:, 2 * p:2 * p + 2, i], ps[:, at:at + 2, 0:(i + 1) * P], AX_X,
                                  ALU.max, negate=True).then_inc(c.s_max, 1)

            def copy_turned(b, p, a, u):
                col, w = unit_columns(u)
                dve.wait_ge(c.xp_ps, nth(b, 3 * HEADS, 6 * p + 3 * a + u + 1))
                dve.wait_ge(c.ob_ps, nth(b, PAIRS, p - 1))
                dve.tensor_copy(pt_at(p, a)[:, col:col + w], ps[:, unit_bank(a, u), 0:w]).then_inc(c.xp_dve, 1)

            def reciprocals(b, p):
                heads = slice((2 * p) % HEADS, (2 * p) % HEADS + 2)
                dve.wait_ge(c.s_exp, nth(b, 2 * SCORES, 8 * p + 8))
                dve.wait_ge(c.wide_ok, nth(b, PAIRS, p))
                dve.tensor_tensor(c.den_b[:], c.sum_b[:, heads, :],
                                  c.ghost[:, heads].rearrange("p (a b) -> p a b", b=1)
                                  .broadcast_to([P, 2, TILES]), ALU.add).then_inc(c.den_ok, 1)
                dve.wait_ge(c.den_ok, nth(b, PAIRS, p + 1))
                dve.reciprocal(c.inv_b[:], c.den_b[:]).then_inc(c.inv_ok, 1)

            def finish(b, p):
                dve.wait_ge(c.ob_ps, nth(b, PAIRS, p + 1))
                dve.wait_ge(c.inv_sb, nth(b, PAIRS, p + 1))
                if p == 0:
                    dve.wait_ge(c.wob_ps, nth(b, 1, 0))
                dve.tensor_tensor(out_at(p), ps[:, 6, :], c.inv_chan[:], ALU.mult).then_inc(c.ob_sb, 1)

            def keep_values(b, n):
                kt, half = divmod(n, 2)
                dve.wait_ge(c.vb_ps, nth(b, 2 * TILES, n + 1))
                if n == 0:
                    dve.wait_ge(c.ob_ps, nth(b, PAIRS, 0))
                dve.tensor_tensor(c.v_b[:, kt, half * S:(half + 1) * S], ps[:, 4 + n % 2, :],
                                  c.bvb[:, half * S:(half + 1) * S], ALU.add).then_inc(c.vb_ok, 1)

            def add_output(b):
                dve.wait_ge(c.wob_ps, nth(b, 1, 0))
                dve.wait_ge(c.x_bias, B + b)
                x_b = c.x_res[:, bass.ds((b - 1) * TILES, TILES), :]
                dve.tensor_tensor(x_b, ps[:, 6, :].rearrange("p (t d) -> p t d", t=TILES), x_b, ALU.add)\
                   .then_inc(c.b_added, 1)

            def batch(b, prev, own):
                if own:
                    ln_statistics(c, dve, 2, b)
                if prev:
                    copy_turned(b, -1, 0, 1)
                    finish(b, -3)
                if own:
                    ln_normalise(c, dve, 2, b)
                if prev:
                    reciprocals(b, -1)
                    copy_turned(b, -1, 0, 2)
                if own:
                    dve.wait_ge(c.xn_hi_ok, B + b + 1)
                    dve.tensor_tensor(c.xn_lo[:], ps[:, 2, :], c.xn_hi[:].bitcast(F32), ALU.subtract)\
                       .then_inc(c.xn_lo_ok, 1)
                if prev:
                    copy_turned(b, -1, 1, 1)
                if own:
                    low(b, 0, 0, 0, c.qb_hi, c.qb_lo)
                if prev:
                    finish(b, -2)
                    copy_turned(b, -1, 1, 2)
                if own:
                    low(b, 0, 1, 1, c.kb_hi, c.kb_lo)
                if prev and not own:
                    finish(b, -1)
                    add_output(b)
                if not own:
                    return
                for p in range(PAIRS):
                    maxima(b, p, 0)
                    if p >= 3:
                        finish(b, p - 3)
                    elif p == 0 and prev:
                        finish(b, -1)
                    if p + 1 < PAIRS:
                        low(b, p + 1, 0, 7, c.qb_hi, c.qb_lo)
                    if p == 0:
                        keep_values(b, 0)
                        keep_values(b, 1)
                    else:
                        copy_turned(b, p - 1, 0, 1)
                    maxima(b, p, 1)
                    if p + 1 < PAIRS:
                        low(b, p + 1, 1, 7, c.kb_hi, c.kb_lo)
                    if p == 0:
                        keep_values(b, 2)
                        keep_values(b, 3)
                    else:
                        copy_turned(b, p - 1, 0, 2)
                        reciprocals(b, p - 1)
                    maxima(b, p, 2)
                    if p == 0:
                        keep_values(b, 4)
                        keep_values(b, 5)
                    else:
                        copy_turned(b, p - 1, 1, 1)
                    maxima(b, p, 3)
                    if p == 0:
                        keep_values(b, 6)
                        keep_values(b, 7)
                    else:
                        copy_turned(b, p - 1, 1, 2)
                    if p == 1 and prev:
                        add_output(b)

            each_batch(dve, batch)

        @block.scalar
        def _(act):
            def high(b, p, which, bank, ps_ready, done):
                act.wait_ge(ps_ready, nth(b, PAIRS, p + 1))
                act.wait_ge(c.s_ps, nth(b, SCORES, TILES * (p - 1)))
                act.activation(part(p, 2 * which), ps[:, bank, :], ACT.Identity, bias=c.bqkb[:, which, p:p + 1])\
                   .then_inc(done, 1)

            def exponentials(b, p, i):
                w = (i + 1) * P
                act.wait_ge(c.s_max, nth(b, SCORES, TILES * p + i + 1))
                if i == 0:
                    act.wait_ge(c.xp_ps, nth(b, 3 * HEADS, 6 * (p - 1)))
                    if p == 0:
                        act.wait_ge(c.den_ok, nth(b, PAIRS, 0))
                for a in range(2):
                    h = 2 * p + a
                    act.activation(p_at(p, a)[:, ROW_AT[i]:ROW_AT[i] + w], ps[:, 2 * (i % 2) + a, 0:w], ACT.Exp,
                                   bias=c.neg_max_b[:, h, i:i + 1], accum_out=c.sum_b[:, h, i:i + 1])\
                       .then_inc(c.s_exp, 1)

            def copy_turned(b, p, a):
                act.wait_ge(c.xp_ps, nth(b, 3 * HEADS, 6 * p + 3 * a + 1))
                act.wait_ge(c.ob_ps, nth(b, PAIRS, p - 1))
                act.activation(pt_at(p, a)[:, 0:S], ps[:, unit_bank(a, 0), :], ACT.Copy).then_inc(c.xp_act, 1)

            def reciprocal_rows(b, p):
                act.wait_ge(c.inv_turned, nth(b, PAIRS, p + 1))
                act.wait_ge(c.ob_sb, nth(b, PAIRS, p))
                act.activation(c.inv_chan[:], ps[:, 7, :], ACT.Copy).then_inc(c.inv_sb, 1)

            def batch(b, prev, own):
                if prev:
                    copy_turned(b, -1, 0)
                    reciprocal_rows(b, -2)
                if own:
                    act.wait_ge(c.ln_turned, 2 * B + b + 1)
                    act.wait_ge(c.vb_ps, nth(b, 2 * TILES, 0))
                    act.wait_ge(c.kb_ps, nth(b, PAIRS, 0))
                    act.activation(c.xn_hi[:], ps[:, 2, :], ACT.Copy).then_inc(c.xn_hi_ok, 1)
                if prev:
                    copy_turned(b, -1, 1)
                if own:
                    high(b, 0, 0, 0, c.qb_ps, c.qb_hi)
                    high(b, 0, 1, 1, c.kb_ps, c.kb_hi)
                if prev:
                    reciprocal_rows(b, -1)
                if not own:
                    return
                for p in range(PAIRS):
                    exponentials(b, p, 0)
                    if p + 1 < PAIRS:
                        high(b, p + 1, 0, 7, c.qb_ps, c.qb_hi)
                    if p >= 1:
                        copy_turned(b, p - 1, 0)
                    exponentials(b, p, 1)
                    if p + 1 < PAIRS:
                        high(b, p + 1, 1, 7, c.kb_ps, c.kb_hi)
                    exponentials(b, p, 2)
                    if p >= 1:
                        copy_turned(b, p - 1, 1)
                    if p >= 2:
                        reciprocal_rows(b, p - 2)
                    exponentials(b, p, 3)

            each_batch(act, batch)

        @block.gpsimd
        def _(pool):
            def widen(b, p):
                pool.wait_ge(c.inv_ok, nth(b, PAIRS, p + 1))
                pool.wait_ge(c.inv_turned, nth(b, PAIRS, p))
                pool.tensor_tensor(c.inv_wide[:], c.inv_b[:].rearrange("p a (t d) -> p t a d", d=1)
                                   .broadcast_to([P, TILES, 2, HD_B]),
                                   c.zero[:].rearrange("p (a b d) -> p a b d", a=1, b=1)
                                   .broadcast_to([P, TILES, 2, HD_B]), ALU.add).then_inc(c.wide_ok, 1)

            def batch(b, prev, own):
                if own:
                    ln_pool(c, pool, 2, b)
                if prev:
                    widen(b, -1)
                if own:
                    add_bias(c, pool, 2, b, c.bob)
                    for p in range(PAIRS - 1):
                        widen(b, p)

            each_batch(pool, batch)


def channel_mixing(c, f, out):
    nc, ps = c.nc, c.ps
    l = 2 * f + 1
    xt, dx, xr, xk, relu_k, k_act, tanh_r, gated = [c.probs[:, n // 2, S * 2 * (n % 2):S * 2 * (n % 2) + S + 1]
                                                    for n in range(8)]
    dx, xr, xk, relu_k, k_act, tanh_r, gated = [tile[:, 0:S] for tile in (dx, xr, xk, relu_k, k_act, tanh_r, gated)]

    with nc.Block() as block:
        @block.tensor
        def _(pe):
            def batch(b, prev, own):
                k = f * B + b
                if own:
                    pe.wait_ge(c.xt_ok, k)
                    ln_tensor(c, pe, l, b, 0)
                if prev:
                    pe.wait_ge(c.kact_ok, k)
                    pe.wait_ge(c.gated_ok, k - 1 if f else nth(b, 1, -1))
                    for t in range(TILES):
                        mm = pe.matmul(ps[:, 3, t * P:(t + 1) * P], k_act[:, t * P:(t + 1) * P], c.wv[:],
                                       start=True, stop=True)
                    mm.then_inc(c.v_ps, 1)
                if own:
                    pe.wait_ge(c.xk_ok, k + 1)
                    pe.wait_ge(c.kact_ok, k)
                    pe.matmul(ps[:, 2, :], c.wk[:], xk, start=True, stop=True).then_inc(c.k_ps, 1)
                    pe.wait_ge(c.xr_ok, k + 1)
                    pe.wait_ge(c.r_tanh, k)
                    for t in range(TILES):
                        mm = pe.matmul(ps[:, 1, t * P:(t + 1) * P], xr[:, t * P:(t + 1) * P], c.wr[:],
                                       start=True, stop=True)
                    mm.then_inc(c.r_ps, 1)

            each_batch(pe, batch)

        @block.vector
        def _(dve):
            dve.memset(xt[:, 0:1], 0.0).then_inc(c.xt_zero, 1)
            dve.wait_ge(c.xt_zero, f + 1)

            def batch(b, prev, own):
                k = f * B + b
                if own:
                    ln_statistics(c, dve, l, b)
                if prev:
                    dve.wait_ge(c.k_relu, k)
                    dve.wait_ge(c.v_ps, k - 1 if f else nth(b, 1, -1))
                    dve.scalar_tensor_tensor(out=k_act, in0=ps[:, 2, :], scalar=0.0, in1=relu_k,
                                             op0=ALU.max, op1=ALU.mult).then_inc(c.kact_ok, 1)
                if own:
                    ln_normalise(c, dve, l, b)
                if prev:
                    dve.wait_ge(c.r_tanh, k)
                    dve.wait_ge(c.v_ps, k)
                    dve.scalar_tensor_tensor(out=gated, in0=tanh_r, scalar=1.0, in1=ps[:, 3, :],
                                             op0=ALU.add, op1=ALU.mult).then_inc(c.gated_ok, 1)
                if own:
                    dve.wait_ge(c.xt_ok, k + 1)
                    dve.tensor_tensor(dx, xt[:, 1:S + 1], xt[:, 0:S], ALU.subtract).then_inc(c.dx_ok, 1)
                    dve.wait_ge(c.dx_ok, k + 1)
                    dve.wait_ge(c.k_ps, k)
                    dve.scalar_tensor_tensor(out=xk, in0=dx, scalar=c.mu[:, 1:2], in1=xt[:, 0:S],
                                             op0=ALU.mult, op1=ALU.add).then_inc(c.xk_ok, 1)
                    dve.wait_ge(c.r_ps, k)
                    dve.scalar_tensor_tensor(out=xr, in0=dx, scalar=c.mu[:, 0:1], in1=xt[:, 0:S],
                                             op0=ALU.mult, op1=ALU.add).then_inc(c.xr_ok, 1)
                if prev:
                    dve.wait_ge(c.gated_ok, k)
                    x_b = c.x_res[:, bass.ds((b - 1) * TILES, TILES), :]
                    dve.scalar_tensor_tensor(out=x_b, in0=gated.rearrange("p (t d) -> p t d", t=TILES),
                                             scalar=0.5, in1=x_b, op0=ALU.mult, op1=ALU.add).then_inc(c.f_added, 1)

            each_batch(dve, batch)

        @block.scalar
        def _(act):
            def batch(b, prev, own):
                k = f * B + b
                if own:
                    act.wait_ge(c.ln_turned, l * B + b + 1)
                    act.wait_ge(c.xr_ok, k)
                    act.activation(xt[:, 1:S + 1], ps[:, 0, :], ACT.Copy).then_inc(c.xt_ok, 1)
                    act.wait_ge(c.k_ps, k + 1)
                    act.wait_ge(c.kact_ok, k)
                    act.activation(relu_k, ps[:, 2, :], ACT.Relu).then_inc(c.k_relu, 1)
                    act.wait_ge(c.r_ps, k + 1)
                    act.wait_ge(c.gated_ok, k)
                    act.activation(tanh_r, ps[:, 1, :], ACT.Tanh, scale=0.5).then_inc(c.r_tanh, 1)

            each_batch(act, batch)

        @block.gpsimd
        def _(pool):
            def batch(b, prev, own):
                if own:
                    ln_pool(c, pool, l, b)

            each_batch(pool, batch)

        if out is not None:
            @block.sync
            def _(sp):
                def batch(b, prev, own):
                    if prev:
                        sp.wait_ge(c.f_added, f * B + b)
                        sp.dma_start(out[bass.ds(b - 1, 1), :, :].rearrange("a (t p) d -> p (a t) d", p=P),
                                     c.x_res[:, bass.ds((b - 1) * TILES, TILES), :]).then_inc(c.out_stored, 16)

                each_batch(sp, batch)
                sp.wait_ge(c.out_stored, B * 16)


def build(nc, d, out):
    with ExitStack() as ctx:
        c = Chip(nc, ctx)
        memory(c)
        semaphores(c)
        setup(c, d)
        attention_a(c)
        channel_mixing(c, 0, None)
        attention_b(c)
        channel_mixing(c, 1, out)


def kernel(**inputs):
    import numpy as np
    import concourse.bacc as bacc
    from concourse.bass_utils import run_bass_kernel_spmd

    a = {k: np.asarray(v) for k, v in inputs.items()}

    def stacked(w):
        t = w.T.reshape(P, GROUPS, BLK)
        return np.concatenate([t, t, t, np.zeros_like(t)], axis=2)

    def stacked_bias(v, fill):
        t = v.reshape(GROUPS, BLK).T
        return np.concatenate([t, t, t, np.full_like(t, fill)], axis=0)

    rows = np.arange(P)
    block, at = rows // BLK, rows % BLK
    head_mask = np.stack([np.where(block < 3, at // HD_A == j, at // 2 == j) for j in range(GROUP)], axis=1)
    causal = np.where(rows[None, :] > rows[:, None], -1e30, 0.0)
    arrays = {
        "x": a["L0_attn_a_x"],
        "wqa": stacked(a["L0_attn_a_Wq"]), "wka": stacked(a["L0_attn_a_Wk"]),
        "wva": a["L0_attn_a_Wv"].T, "woa": a["L0_attn_a_Wo"].T,
        "bqa": stacked_bias(a["L0_attn_a_bq"], 0.0), "bka": stacked_bias(a["L0_attn_a_bk"], 1.0),
        "bva": a["L0_attn_a_bv"], "boa": a["L0_attn_a_bo"],
        "wb": a["L0_attn_b_Wqkv_w"].T, "wob": a["L0_attn_b_Wo_w"].T,
        "bqkb": a["L0_attn_b_Wqkv_b"][:2 * HEADS * HD_B].reshape(2, PAIRS, P).transpose(2, 0, 1),
        "bvb": a["L0_attn_b_Wqkv_b"][2 * HEADS * HD_B:], "bob": a["L0_attn_b_Wo_b"],
        "ghost": a["L0_attn_b_ghost"],
        "wr": a["L0_ffn_W_r"].T, "wk": a["L0_ffn_W_k"].T, "wv": a["L0_ffn_W_v"].T,
        "mu": np.stack([a["L0_ffn_mu_r"], a["L0_ffn_mu_k"]], axis=1),
        "ident": np.eye(P, dtype=np.float32), "head_mask": head_mask.astype(np.float32),
        "causal": causal.astype(np.float32),
    }
    arrays = {k: np.ascontiguousarray(v) for k, v in arrays.items()}

    nc = bacc.Bacc("TRN2", target_bir_lowering=False, num_devices=1)
    d = {k: nc.dram_tensor("in_" + k, v.shape, mybir.dt.from_np(v.dtype), kind="ExternalInput").ap()
         for k, v in arrays.items()}
    out = nc.dram_tensor("out", (B, S, P), F32, kind="ExternalOutput").ap()
    build(nc, d, out)
    r = run_bass_kernel_spmd(nc, [{"in_" + k: v for k, v in arrays.items()}], core_ids=[0])
    return r.results[0]["out"]
```

```python
from contextlib import ExitStack

import concourse.bass as bass
from concourse import mybir

F32 = mybir.dt.float32
F32R = mybir.dt.float32r
BF16 = mybir.dt.bfloat16
ALU = mybir.AluOpType
ACT = mybir.ActivationFunctionType
AX_X = mybir.AxisListType.X

P = 128
B = 4
S = 512
TILES = S // P
EPS = 1e-5

HEADS = 16
HD_A = P // HEADS
GROUP = 4
GROUPS = HEADS // GROUP
BLK = GROUP * HD_A
SCALE_A = HD_A ** -0.5
M_ROWS = 3 * BLK

HD_B = 64
PAIRS = HEADS // 2
SCALE_B = HD_B ** -0.5
CAUSAL = TILES * (TILES + 1) // 2 * P
ROW_AT = [P * i * (i + 1) // 2 for i in range(TILES + 1)]
COL_AT = [sum((TILES - k) * P for k in range(n)) for n in range(TILES + 1)]
UNITS = [(0,), (1,), (2, 3)]


def nth(b, per, n):
    count = b * per + n
    return max(count, 0) if isinstance(b, int) else count


def each_batch(engine, batch):
    batch(0, False, True, True)
    with engine.Fori(1, B - 1) as b:
        batch(b, True, True, True)
    batch(B - 1, True, True, False)
    batch(B, True, False, False)


class Chip:

    def __init__(self, nc, ctx):
        self.nc, self.ctx = nc, ctx

    def sb(self, name, shape, dt=F32):
        return self.ctx.enter_context(self.nc.sbuf_tensor(name, shape, dt))

    def sems(self, *names):
        return [self.ctx.enter_context(self.nc.semaphore(n)) for n in names]


def memory(c):
    c.ps = c.ctx.enter_context(c.nc.psum_tensor("ps", [P, 8, 512], F32))
    c.x_res = c.sb("x_res", [P, B * TILES, P])
    c.ident = c.sb("ident", [P, P])
    c.ident_bf = c.sb("ident_bf", [P, P], BF16)
    c.causal_bf = c.sb("causal_bf", [P, P], BF16)
    c.head_mask = c.sb("head_mask", [P, GROUP])
    c.minus_half = c.sb("minus_half", [P, TILES])
    c.eps = c.sb("eps", [P, TILES])
    c.zero = c.sb("zero", [P, 1])
    c.ln_carry = c.sb("ln_carry", [P, 1])
    c.wqa_hi = c.sb("wqa_hi", [P, GROUPS, P], F32R)
    c.wqa_lo = c.sb("wqa_lo", [P, GROUPS, P], F32R)
    c.wka_hi = c.sb("wka_hi", [P, GROUPS, P], F32R)
    c.wka_lo = c.sb("wka_lo", [P, GROUPS, P], F32R)
    c.wva_hi = c.sb("wva_hi", [P, P], F32R)
    c.wva_lo = c.sb("wva_lo", [P, P], F32R)
    c.woa = c.sb("woa", [P, P])
    c.bqa = c.sb("bqa", [P, GROUPS])
    c.bka = c.sb("bka", [P, GROUPS])
    c.bva = c.sb("bva", [P, P])
    c.boa = c.sb("boa", [P, P])
    c.wb_hi = c.sb("wb_hi", [P, 3 * HEADS * HD_B], F32R)
    c.wb_lo = c.sb("wb_lo", [P, 3 * HEADS * HD_B], F32R)
    c.wob = c.sb("wob", [P, PAIRS, P])
    c.bqkb = c.sb("bqkb", [P, 2, PAIRS])
    c.bvb = c.sb("bvb", [P, HEADS * HD_B])
    c.bob = c.sb("bob", [P, P])
    c.ghost = c.sb("ghost", [P, HEADS])
    c.wr = c.sb("wr", [P, P])
    c.wk = c.sb("wk", [P, P])
    c.wv = c.sb("wv", [P, P])
    c.mu = c.sb("mu", [P, 2])
    c.stats = c.sb("stats", [P, TILES, 6])
    c.mean_var = c.sb("mean_var", [P, TILES, 2])
    c.var_eps = c.sb("var_eps", [P, TILES])
    c.rstd = c.sb("rstd", [P, TILES])
    c.xn = c.sb("xn", [P, TILES, P])
    c.xn_hi = c.sb("xn_hi", [P, S], F32R)
    c.xn_lo = c.sb("xn_lo", [P, S], F32R)
    c.v_a = c.sb("v_a", [P, TILES, HEADS, BLK])
    c.q_stack = c.sb("q_stack", [P, GROUPS, S], F32R)
    c.k_group = c.sb("k_group", [P, S], F32R)
    c.stack = c.sb("stack", [P, 8, S], F32R)
    c.neg_max = c.sb("neg_max", [P, GROUP, TILES])
    c.max_cols = c.sb("max_cols", [P, TILES, BLK // 2, 2])
    c.probs = c.sb("probs", [P, 8, TILES * S])
    c.o_sb = c.sb("o_sb", [P, S])
    c.inv_a = c.sb("inv_a", [P, TILES, GROUP])
    c.a_tok = c.sb("a_tok", [P, TILES, P])
    c.a_chan = c.sb("a_chan", [P, S])
    c.xt = c.sb("xt", [P, S + 1])
    c.causal = c.sb("causal", [P, P])
    c.v_b = c.sb("v_b", [P, TILES, HEADS * HD_B])
    c.neg_max_b = c.sb("neg_max_b", [P, HEADS, TILES])
    c.sum_b = c.sb("sum_b", [P, HEADS, TILES])
    c.den_b = c.sb("den_b", [P, 2, TILES])
    c.inv_b = c.sb("inv_b", [P, 2, TILES])
    c.inv_wide = c.sb("inv_wide", [P, TILES, 2, HD_B])
    c.inv_chan = c.sb("inv_chan", [P, S])


def semaphores(c):
    c.x0_loaded, c.ident_loaded, c.bias_loaded, c.bva_loaded = c.sems(
        "x0_loaded", "ident_loaded", "bias_loaded", "bva_loaded")
    c.ka_loaded, c.qa_loaded, c.va_loaded, c.x_loaded, c.boa_loaded, c.woa_loaded = c.sems(
        "ka_loaded", "qa_loaded", "va_loaded", "x_loaded", "boa_loaded", "woa_loaded")
    c.wb_loaded, c.later_loaded, c.out_stored = c.sems("wb_loaded", "later_loaded", "out_stored")
    c.w_hi, c.w_lo, c.set_const, c.wb_scaled, c.wb_high, c.wb_low = c.sems(
        "w_hi", "w_lo", "set_const", "wb_scaled", "wb_high", "wb_low")
    c.ln_stats, c.ln_mean, c.ln_eps, c.ln_rstd, c.ln_xn, c.ln_turned = c.sems(
        "ln_stats", "ln_mean", "ln_eps", "ln_rstd", "ln_xn", "ln_turned")
    c.xn_hi_ok, c.xn_lo_ok, c.x_bias = c.sems(
        "xn_hi_ok", "xn_lo_ok", "x_bias")
    c.va_ps, c.va_ok, c.ka_ps, c.ka_hi, c.ka_lo, c.km_dve, c.km_act = c.sems(
        "va_ps", "va_ok", "ka_ps", "ka_hi", "ka_lo", "km_dve", "km_act")
    c.qa_ps, c.qa_hi, c.qa_lo, c.n_ps, c.n_max, c.m_hi = c.sems(
        "qa_ps", "qa_hi", "qa_lo", "n_ps", "n_max", "m_hi")
    c.m_lo, c.m_turned, c.m_set, c.t_ps, c.t_exp, c.oa_ps = c.sems(
        "m_lo", "m_turned", "m_set", "t_ps", "t_exp", "oa_ps")
    c.oa_sb, c.oa_turned, c.oa_inv, c.oa_tok, c.at_turned, c.at_sb = c.sems(
        "oa_sb", "oa_turned", "oa_inv", "oa_tok", "at_turned", "at_sb")
    c.woa_ps, c.a_added = c.sems(
        "woa_ps", "a_added")
    c.vb_ps, c.vb_ok, c.qb_ps, c.qb_hi, c.qb_lo, c.kb_ps = c.sems(
        "vb_ps", "vb_ok", "qb_ps", "qb_hi", "qb_lo", "kb_ps")
    c.kb_hi, c.kb_lo, c.s_ps, c.s_max, c.s_exp, c.xp_ps = c.sems(
        "kb_hi", "kb_lo", "s_ps", "s_max", "s_exp", "xp_ps")
    c.xp_act, c.xp_dve, c.den_ok, c.inv_ok, c.wide_ok, c.inv_turned = c.sems(
        "xp_act", "xp_dve", "den_ok", "inv_ok", "wide_ok", "inv_turned")
    c.inv_sb, c.ob_ps, c.ob_sb, c.wob_ps, c.b_added = c.sems(
        "inv_sb", "ob_ps", "ob_sb", "wob_ps", "b_added")
    c.xt_ok, c.dx_ok, c.xr_ok, c.xk_ok, c.r_ps, c.k_ps = c.sems(
        "xt_ok", "dx_ok", "xr_ok", "xk_ok", "r_ps", "k_ps")
    c.r_tanh, c.k_relu, c.kact_ok, c.v_ps, c.gated_ok, c.f_added = c.sems(
        "r_tanh", "k_relu", "kact_ok", "v_ps", "gated_ok", "f_added")


def raw_weights(c):
    raw = c.probs[:].rearrange("p s n -> p (s n)")
    n_a = GROUPS * P
    return (raw[:, 0:n_a].rearrange("p (g n) -> p g n", g=GROUPS),
            raw[:, n_a:2 * n_a].rearrange("p (g n) -> p g n", g=GROUPS), raw[:, 2 * n_a:2 * n_a + P])


def first_loads_sync(c, sp, d):
    raw_ka, raw_qa, raw_va = raw_weights(c)
    sp.dma_start(c.x_res[:, 0:TILES, :], d["x"][0].rearrange("(t p) d -> p t d", p=P)).then_inc(c.x0_loaded, 16)
    sp.dma_start(raw_ka, d["wka"]).then_inc(c.ka_loaded, 16)
    sp.dma_start(raw_qa, d["wqa"]).then_inc(c.qa_loaded, 16)
    sp.dma_start(raw_va, d["wva"]).then_inc(c.va_loaded, 16)
    sp.dma_start(c.bva[:], d["bva"].partition_broadcast(P)).then_inc(c.bva_loaded, 16)
    sp.dma_start(c.boa[:], d["boa"].partition_broadcast(P)).then_inc(c.boa_loaded, 16)
    sp.dma_start(c.woa[:], d["woa"]).then_inc(c.woa_loaded, 16)
    for b in range(1, B):
        sp.dma_start(c.x_res[:, b * TILES:(b + 1) * TILES, :],
                     d["x"][b].rearrange("(t p) d -> p t d", p=P)).then_inc(c.x_loaded, 16)


def first_loads_scalar(c, act, d):
    act.dma_start(c.ident[:], d["ident"]).then_inc(c.ident_loaded, 16)
    for dst, src in ((c.bka[:], d["bka"]), (c.head_mask[:], d["head_mask"]), (c.bqa[:], d["bqa"])):
        act.dma_start(dst, src).then_inc(c.bias_loaded, 16)


def set_constants(c, pool):
    pool.memset(c.minus_half[:], -0.5).then_inc(c.set_const, 1)
    pool.memset(c.eps[:], EPS).then_inc(c.set_const, 1)
    pool.memset(c.zero[:], 0.0).then_inc(c.set_const, 1)
    pool.memset(c.xt[:, 0:1], 0.0).then_inc(c.set_const, 1)
    pool.memset(c.max_cols[:], 0.0).then_inc(c.set_const, 1)
    pool.memset(c.v_a[:], 0.0).then_inc(c.set_const, 1)
    pool.wait_ge(c.set_const, 6)
    pool.memset(c.v_a[:, :, :, HD_A:HD_A + 1], 1.0).then_inc(c.set_const, 1)


def split_weights(c, dve, hi, lo, w, n):
    dve.tensor_copy(hi, w).then_inc(c.w_hi, 1)
    dve.wait_ge(c.w_hi, n)
    dve.tensor_tensor(lo, w, hi.bitcast(F32), ALU.subtract).then_inc(c.w_lo, 1)


def later_loads(c, sp, d):
    n = 0
    for dst, src in ((c.v_b[:].rearrange("p t n -> p (t n)")[:, 0:3 * HEADS * HD_B], d["wb"]),
                     (c.causal[:], d["causal"]), (c.bqkb[:], d["bqkb"])):
        sp.dma_start(dst, src).then_inc(c.wb_loaded, 16)
    for dst, src in ((c.wr[:], d["wr"]), (c.wk[:], d["wk"]), (c.wv[:], d["wv"]), (c.mu[:], d["mu"]),
                     (c.ghost[:], d["ghost"].partition_broadcast(P)), (c.bob[:], d["bob"].partition_broadcast(P)),
                     (c.bvb[:], d["bvb"].partition_broadcast(P)),
                     (c.wob[:], d["wob"].rearrange("(h p) d -> p h d", p=P))):
        sp.dma_start(dst, src).then_inc(c.later_loaded, 16)
        n += 16
    sp.wait_ge(c.later_loaded, n)


def split_later_weights(c, pool):
    raw = c.v_b[:].rearrange("p t n -> p (t n)")
    n_q = HEADS * HD_B
    pool.wait_ge(c.ident_loaded, 16)
    pool.wait_ge(c.wb_loaded, 3 * 16)
    pool.tensor_scalar(raw[:, 0:n_q], raw[:, 0:n_q], SCALE_B, None, ALU.mult).then_inc(c.wb_scaled, 1)
    pool.tensor_scalar(c.bqkb[:, 0, :], c.bqkb[:, 0, :], SCALE_B, None, ALU.mult).then_inc(c.wb_scaled, 1)
    pool.tensor_copy(c.ident_bf[:], c.ident[:]).then_inc(c.wb_scaled, 1)
    pool.tensor_copy(c.causal_bf[:], c.causal[:]).then_inc(c.wb_scaled, 1)
    pool.wait_ge(c.wb_scaled, 4)
    for n in range(3):
        w = slice(n * n_q, (n + 1) * n_q)
        pool.tensor_copy(c.wb_hi[:, w], raw[:, w]).then_inc(c.wb_high, 1)
        pool.wait_ge(c.wb_high, n + 1)
        pool.tensor_tensor(c.wb_lo[:, w], raw[:, w], c.wb_hi[:, w].bitcast(F32), ALU.subtract)\
            .then_inc(c.wb_low, 1)


def ln_statistics(c, dve, l, b):
    k = l * B + b
    for t in range(TILES):
        dve.bn_stats(c.stats[:, t, :], c.x_res[:, bass.ds(b * TILES + t, 1), :]
                     .rearrange("p a d -> p (a d)")).then_inc(c.ln_stats, 1)
    dve.wait_ge(c.ln_eps, k)
    dve.wait_ge(c.ln_stats, nth(k, TILES, TILES))
    dve.memset(c.ln_carry[:], 0.0)
    for t in range(TILES):
        dve.bn_aggr(c.mean_var[:, t, :], c.stats[:, t, :]).then_inc(c.ln_mean, 1)


def ln_normalise(c, dve, l, b):
    k = l * B + b
    dve.wait_ge(c.ln_rstd, k + 1)
    dve.wait_ge(c.ln_turned, k)
    for t in range(TILES):
        dve.tensor_scalar(c.xn[:, t, :], c.x_res[:, bass.ds(b * TILES + t, 1), :]
                          .rearrange("p a d -> p (a d)"), c.mean_var[:, t, 0:1], c.rstd[:, t:t + 1],
                          ALU.subtract, ALU.mult).then_inc(c.ln_xn, 1)


def ln_pool(c, pool, l, b):
    k = l * B + b
    pool.wait_ge(c.ln_mean, nth(k, TILES, TILES))
    pool.tensor_tensor(c.var_eps[:], c.mean_var[:, :, 1], c.eps[:], ALU.add).then_inc(c.ln_eps, 1)
    pool.wait_ge(c.ln_eps, k + 1)
    pool.wait_ge(c.ln_xn, nth(k, TILES, 0))
    pool.tensor_tensor(c.rstd[:], c.var_eps[:], c.minus_half[:], ALU.pow).then_inc(c.ln_rstd, 1)


def ln_tensor(c, pe, l, b, bank):
    k = l * B + b
    for t in range(TILES):
        pe.wait_ge(c.ln_xn, nth(k, TILES, t + 1))
        mm = pe.transpose(c.ps[:, bank, t * P:(t + 1) * P], c.xn[:, t, :], c.ident[:])
    mm.then_inc(c.ln_turned, 1)


def three_passes(pe, out, lhs, rhs):
    (lh, ll), (rh, rl) = lhs, rhs
    pe.matmul(out, lh, rh, start=True, stop=False)
    pe.matmul(out, ll, rh, start=False, stop=False)
    return pe.matmul(out, lh, rl, start=False, stop=True)


def add_bias(c, pool, l, b, bias):
    pool.wait_ge(c.ln_xn, nth(l * B + b, TILES, TILES))
    x_b = c.x_res[:, bass.ds(b * TILES, TILES), :]
    pool.tensor_tensor(x_b, x_b, bias[:].rearrange("p (a d) -> p a d", a=1).broadcast_to([P, TILES, P]),
                       ALU.add).then_inc(c.x_bias, 1)


class Mixing:
    def __init__(self, c, f):
        self.c, self.f, self.l = c, f, 2 * f + 1
        if f == 0:
            flat = c.v_b[:].rearrange("p t n -> p (t n)")
            at = [n * S for n in range(7)]
        else:
            flat = c.probs[:].rearrange("p s n -> p (s n)")
            at = [n * S for n in range(4)] + [8 * CAUSAL + (PAIRS + n) * S for n in range(3)]
        self.dx, self.xr, self.xk, self.gated, self.relu_k, self.k_act, self.tanh_r = \
            [flat[:, n:n + S] for n in at]

    def norm_and_value(self, pe, b, prev=True, own=True):
        c, ps, k = self.c, self.c.ps, self.f * B + b
        if own:
            pe.wait_ge(c.r_tanh, k)
            ln_tensor(c, pe, self.l, b, 0)
        if prev:
            pe.wait_ge(c.kact_ok, k)
            for t in range(TILES):
                mm = pe.matmul(ps[:, 1, t * P:(t + 1) * P], self.k_act[:, t * P:(t + 1) * P], c.wv[:],
                               start=True, stop=True)
            mm.then_inc(c.v_ps, 1)

    def key_and_receptance(self, pe, b):
        c, ps, k = self.c, self.c.ps, self.f * B + b
        pe.wait_ge(c.gated_ok, k)
        pe.wait_ge(c.xk_ok, k + 1)
        pe.matmul(ps[:, 1, :], c.wk[:], self.xk, start=True, stop=True).then_inc(c.k_ps, 1)
        pe.wait_ge(c.xr_ok, k + 1)
        pe.wait_ge(c.xt_ok, k + 1)
        for t in range(TILES):
            mm = pe.matmul(ps[:, 0, t * P:(t + 1) * P], self.xr[:, t * P:(t + 1) * P], c.wr[:],
                           start=True, stop=True)
        mm.then_inc(c.r_ps, 1)

    def statistics(self, dve, b):
        if self.f == 0:
            dve.wait_ge(self.c.a_added, b + 1)
        else:
            dve.wait_ge(self.c.b_added, TILES * (b + 1))
        ln_statistics(self.c, dve, self.l, b)

    def vector(self, dve, b, prev=True, own=True, more=True):
        c, ps, k = self.c, self.c.ps, self.f * B + b
        xt, dx, gated = c.xt, self.dx, self.gated
        if own:
            ln_normalise(c, dve, self.l, b)
        if more:
            self.statistics(dve, b + 1)
        if own:
            dve.wait_ge(c.xt_ok, k + 1)
            dve.wait_ge(c.xr_ok, k)
            dve.tensor_tensor(dx, xt[:, 1:S + 1], xt[:, 0:S], ALU.subtract).then_inc(c.dx_ok, 1)
        if prev:
            dve.wait_ge(c.r_tanh, k)
            dve.wait_ge(c.v_ps, k)
            dve.wait_ge(c.f_added, k - 1)
            dve.scalar_tensor_tensor(out=gated, in0=self.tanh_r, scalar=1.0, in1=ps[:, 1, :],
                                     op0=ALU.add, op1=ALU.mult).then_inc(c.gated_ok, 1)
        if own:
            dve.wait_ge(c.dx_ok, k + 1)
            dve.wait_ge(c.k_ps, k)
            dve.scalar_tensor_tensor(out=self.xk, in0=dx, scalar=c.mu[:, 1:2], in1=xt[:, 0:S],
                                     op0=ALU.mult, op1=ALU.add).then_inc(c.xk_ok, 1)
            dve.wait_ge(c.r_ps, k)
            dve.scalar_tensor_tensor(out=self.xr, in0=dx, scalar=c.mu[:, 0:1], in1=xt[:, 0:S],
                                     op0=ALU.mult, op1=ALU.add).then_inc(c.xr_ok, 1)
        if prev:
            dve.wait_ge(c.gated_ok, k)
            x_b = c.x_res[:, (b - 1) * TILES:b * TILES, :]
            dve.scalar_tensor_tensor(out=x_b, in0=gated.rearrange("p (t d) -> p t d", t=TILES),
                                     scalar=0.5, in1=x_b, op0=ALU.mult, op1=ALU.add).then_inc(c.f_added, 1)

    def keep_input(self, act, b):
        c, ps, k = self.c, self.c.ps, self.f * B + b
        act.wait_ge(c.ln_turned, self.l * B + b + 1)
        act.wait_ge(c.xr_ok, k)
        act.activation(c.xt[:, 1:S + 1], ps[:, 0, :], ACT.Copy).then_inc(c.xt_ok, 1)

    def activations(self, act, b):
        c, ps, k = self.c, self.c.ps, self.f * B + b
        act.wait_ge(c.k_ps, k + 1)
        act.wait_ge(c.kact_ok, k)
        act.activation(self.relu_k, ps[:, 1, :], ACT.Relu).then_inc(c.k_relu, 1)
        act.wait_ge(c.k_relu, k + 1)
        act.wait_ge(c.v_ps, k)
        act.activation(self.k_act, self.relu_k, ACT.Square).then_inc(c.kact_ok, 1)
        act.wait_ge(c.r_ps, k + 1)
        act.wait_ge(c.gated_ok, k)
        act.activation(self.tanh_r, ps[:, 0, :], ACT.Tanh, scale=0.5).then_inc(c.r_tanh, 1)

    def pool(self, pool, b):
        ln_pool(self.c, pool, self.l, b)

    def store(self, sp, out, batches):
        for b in batches:
            sp.wait_ge(self.c.f_added, self.f * B + b + 1)
            sp.dma_start(out[b].rearrange("(t p) d -> p t d", p=P),
                         self.c.x_res[:, b * TILES:(b + 1) * TILES, :]).then_inc(self.c.out_stored, 16)


def last_mixing(c, f, out):
    mix, last = Mixing(c, f), B - 1
    with c.nc.Block() as block:
        @block.tensor
        def _(pe):
            mix.norm_and_value(pe, last)
            mix.key_and_receptance(pe, last)
            mix.norm_and_value(pe, B, own=False)

        @block.vector
        def _(dve):
            mix.statistics(dve, last)
            mix.vector(dve, last, more=False)
            mix.vector(dve, B, own=False, more=False)

        @block.scalar
        def _(act):
            mix.keep_input(act, last)
            mix.activations(act, last)

        @block.gpsimd
        def _(pool):
            mix.pool(pool, last)

        @block.sync
        def _(sp):
            mix.store(sp, out, (B - 2, B - 1))
            sp.wait_ge(c.out_stored, B * 16)


def attention_a(c, d):
    nc, ps = c.nc, c.ps
    MAXIMA = HEADS * TILES
    HALVES = HEADS * 2

    def k_stack(g, j):
        return c.stack[:, GROUP * (g % 2) + j, :]

    def q_stack(g):
        return c.q_stack[:, g % GROUPS, :]

    def probs(g, j):
        return c.probs[:, GROUP * (g % 2) + j, :]

    mix = Mixing(c, 0)

    VALUES_AT = (5, 8, 12, 15)

    NORM_AT = ((0, 5), (1, 5), (1, 13))
    KEY_AT = ((0, 12), (1, 9), (2, 3))

    with nc.Block() as block:
        @block.tensor
        def _(pe):
            def project_k(b, g):
                w = g % GROUPS
                three_passes(pe, ps[:, 7, :], (c.wka_hi[:, w, :], c.wka_lo[:, w, :]), (c.xn_hi[:], c.xn_lo[:]))\
                    .then_inc(c.ka_ps, 1)

            def project_q(b, g, bank=7):
                w = g % GROUPS
                three_passes(pe, ps[:, bank, :], (c.wqa_hi[:, w, :], c.wqa_lo[:, w, :]), (c.xn_hi[:], c.xn_lo[:]))\
                    .then_inc(c.qa_ps, 1)

            def project_values(b):
                pe.wait_ge(c.qa_lo, nth(b, GROUPS, 3))
                for t in range(TILES):
                    tok = slice(t * P, (t + 1) * P)
                    mm = three_passes(pe, ps[:, 7, tok], (c.xn_hi[:, tok], c.xn_lo[:, tok]),
                                      (c.wva_hi[:], c.wva_lo[:]))
                mm.then_inc(c.va_ps, 1)

            def scores(b, g, i):
                j, qt = divmod(i, TILES)
                n = 16 * g + i
                if i == 0:
                    pe.wait_ge(c.qa_lo, nth(b, GROUPS, g + 1))
                if qt == 0 and j == 0:
                    pe.wait_ge(c.km_dve, nth(b, GROUPS, g + 1))
                elif qt == 0:
                    pe.wait_ge(c.km_act, nth(b, HEADS - GROUPS, (GROUP - 1) * g + j))
                pe.wait_ge(c.n_max, nth(b, MAXIMA, n - 1))
                pe.matmul(ps[:, n % 2, :], q_stack(g)[:, qt * P:(qt + 1) * P], k_stack(g, j),
                          start=True, stop=True).then_inc(c.n_ps, 1)

            def turn_maxima(b, g):
                pe.wait_ge(c.m_lo, nth(b, GROUPS, g + 1))
                for qt in range(TILES):
                    mm = pe.transpose(ps[0:BLK, 7, qt * P:(qt + 1) * P],
                                      c.max_cols[:, qt, :, :].rearrange("p a b -> p (a b)"), c.ident[:])
                mm.then_inc(c.m_turned, 1)

            def scores_turned(b, g, i):
                j, kt = divmod(i, TILES)
                half = 8 * g + 2 * j + kt // 2
                if i == 0:
                    pe.wait_ge(c.m_set, nth(b, GROUPS, g + 1))
                if kt % 2 == 0:
                    pe.wait_ge(c.t_exp, nth(b, HALVES, half - 1))
                mm = pe.matmul(ps[:, 2 + 2 * (half % 2) + kt % 2, :], k_stack(g, j)[:, kt * P:(kt + 1) * P],
                               q_stack(g), start=True, stop=True)
                if kt % 2 == 1:
                    mm.then_inc(c.t_ps, 1)

            def times_values(b, g, kt):
                if kt == 0:
                    pe.wait_ge(c.va_ok, nth(b, 1, 1 if g >= 0 else 0))
                    pe.wait_ge(c.t_exp, nth(b, HALVES, 8 * g + 8))
                    pe.wait_ge(c.oa_sb, nth(b, GROUPS, g))
                for j in range(GROUP):
                    mm = pe.matmul(ps[BLK * j:BLK * (j + 1), 6, :], c.v_a[:, kt, (GROUP * g + j) % HEADS, :],
                                   probs(g, j)[:, kt * S:(kt + 1) * S], start=(kt == 0), stop=(kt == TILES - 1))
                if kt == TILES - 1:
                    mm.then_inc(c.oa_ps, 1)

            def turn_output(b, g):
                pe.wait_ge(c.oa_sb, nth(b, GROUPS, g + 1))
                for qt in range(TILES):
                    mm = pe.transpose(ps[:, 7, qt * P:(qt + 1) * P], c.o_sb[:, qt * P:(qt + 1) * P], c.ident[:])
                mm.then_inc(c.oa_turned, 1)

            def turn_batch(b):
                pe.wait_ge(c.oa_tok, nth(b, GROUPS, 0))
                for t in range(TILES):
                    mm = pe.transpose(ps[:, 7, t * P:(t + 1) * P], c.a_tok[:, t, :], c.ident[:])
                mm.then_inc(c.at_turned, 1)

            def output_product(b):
                pe.wait_ge(c.at_sb, nth(b, 1, 0))
                for t in range(TILES):
                    mm = pe.matmul(ps[:, 7, t * P:(t + 1) * P], c.a_chan[:, t * P:(t + 1) * P], c.woa[:],
                                   start=True, stop=True)
                mm.then_inc(c.woa_ps, 1)

            def step(b, s, prev, own, more):
                last = prev if s == 0 else own
                before = own if s >= 2 else prev
                third = own if s == 3 else prev
                following = own and (s < 3 or more)
                maxima_at, output_at, k_at, q_at = (2, 6, 9, 13) if s == 3 else (1, 4, 6, 10)
                for i in range(16):
                    if own:
                        scores(b, s, i)
                    if own and prev and s == 3 and i == 0:
                        output_product(b)
                    if last and i == maxima_at:
                        if not own:
                            pe.wait_ge(c.oa_tok, nth(b, GROUPS, -3))
                        elif s == 2:
                            pe.wait_ge(c.va_ok, nth(b, 1, 1))
                        else:
                            pe.wait_ge(c.qa_lo, nth(b, GROUPS, s + 1))
                            if s == 3:
                                pe.wait_ge(c.a_added, nth(b, 1, 0))
                        turn_maxima(b, s - 1)
                    g, ti = divmod(16 * (s - 1) + i - 3, 16)
                    if own and g >= 0 or prev and g < 0:
                        scores_turned(b, g, ti)
                    if own and more and s == 3 and i == 4:
                        pe.wait_ge(c.m_set, nth(b, GROUPS, s))
                        ln_tensor(c, pe, 0, b + 1, 7)
                    if third and i == output_at:
                        if own and more and s == 3:
                            pe.wait_ge(c.xn_lo_ok, b + 2)
                        elif s == 0 or own:
                            pe.wait_ge(c.m_set, nth(b, GROUPS, s))
                        pe.wait_ge(c.oa_tok, nth(b, GROUPS, s - 3))
                        turn_output(b, s - 3)
                    if following and i == k_at:
                        pe.wait_ge(c.m_set, nth(b, GROUPS, s))
                        pe.wait_ge(c.qa_lo, nth(b, GROUPS, s + 1))
                        pe.wait_ge(c.oa_tok, nth(b, GROUPS, s - 2))
                        project_k(b, s + 1)
                    if following and i == q_at:
                        pe.wait_ge(c.ka_lo, nth(b, GROUPS, s + 2))
                        project_q(b, s + 1)
                    if before and i in VALUES_AT:
                        times_values(b, s - 2, VALUES_AT.index(i))
                    if own and s == 1 and i == 15:
                        project_values(b)
                    if not own and (s, i) in NORM_AT:
                        k = NORM_AT.index((s, i))
                        mix.norm_and_value(pe, k, prev=k > 0)
                    if not own and (s, i) in KEY_AT:
                        mix.key_and_receptance(pe, KEY_AT.index((s, i)))
                    if prev and s == 2 and i == 15:
                        if own:
                            pe.wait_ge(c.qa_lo, nth(b, GROUPS, 4))
                        turn_batch(b)
                if prev and not own and s == 2:
                    output_product(b)

            pe.wait_ge(c.ident_loaded, 16)
            ln_tensor(c, pe, 0, 0, 7)
            pe.wait_ge(c.xn_lo_ok, 1)
            pe.wait_ge(c.w_lo, 3)
            project_k(-1, 4)
            project_q(-1, 4, bank=6)
            pe.wait_ge(c.woa_loaded, 16)
            pe.wait_ge(c.set_const, 7)

            def batch(b, prev, own, more):
                if not own:
                    pe.wait_ge(c.later_loaded, 8 * 16)
                for s in range(GROUPS if own else GROUPS - 1):
                    step(b, s, prev, own, more)

            each_batch(pe, batch)

        @block.vector
        def _(dve):
            def k_low(b, g):
                rows = slice(BLK, 2 * BLK)
                dve.wait_ge(c.ka_hi, nth(b, GROUPS, g + 1))
                dve.scalar_tensor_tensor(out=c.k_group[rows, :], in0=ps[rows, 7, :],
                                         scalar=c.bka[rows, g % GROUPS:g % GROUPS + 1],
                                         in1=c.k_group[rows, :].bitcast(F32), op0=ALU.add, op1=ALU.subtract)\
                   .then_inc(c.ka_lo, 1)

            def q_low(b, g, bank=7):
                rows = slice(2 * BLK, 3 * BLK)
                dve.wait_ge(c.qa_hi, nth(b, GROUPS, g + 1))
                dve.scalar_tensor_tensor(out=q_stack(g)[rows, :], in0=ps[rows, bank, :],
                                         scalar=c.bqa[rows, g % GROUPS:g % GROUPS + 1],
                                         in1=q_stack(g)[rows, :].bitcast(F32),
                                         op0=ALU.add, op1=ALU.subtract).then_inc(c.qa_lo, 1)

            def mask_keys(b, g):
                dve.wait_ge(c.ka_lo, nth(b, GROUPS, g + 1))
                dve.wait_ge(c.t_ps, nth(b, HALVES, 8 * (g - 2) + 2))
                dve.tensor_scalar(k_stack(g, 0), c.k_group[:].bitcast(F32), c.head_mask[:, 0:1], None,
                                  ALU.mult).then_inc(c.km_dve, 1)

            def maximum(b, g, i):
                j, qt = divmod(i, TILES)
                n = 16 * g + i
                dve.wait_ge(c.n_ps, nth(b, MAXIMA, n + 1))
                if i == 0:
                    dve.wait_ge(c.m_lo, nth(b, GROUPS, g))
                dve.tensor_reduce(c.neg_max[:, j, qt:qt + 1], ps[:, n % 2, :], AX_X, ALU.max, negate=True)\
                   .then_inc(c.n_max, 1)

            def split_maxima(b, g):
                nm = c.neg_max[:].rearrange("p j t -> p t j")
                dve.wait_ge(c.n_max, nth(b, MAXIMA, 16 * g + 16))
                dve.wait_ge(c.m_turned, nth(b, GROUPS, g))
                dve.tensor_copy(c.max_cols[:, :, 0:GROUP, 0].bitcast(F32R), nm).then_inc(c.m_hi, 1)
                dve.wait_ge(c.m_hi, nth(b, GROUPS, g + 1))
                dve.tensor_tensor(c.max_cols[:, :, 0:GROUP, 1], nm, c.max_cols[:, :, 0:GROUP, 0],
                                  ALU.subtract).then_inc(c.m_lo, 1)

            def divide(b, g):
                at = BLK * (g % GROUPS)
                o = ps[:, 7, :].rearrange("p (t j d) -> p t j d", t=TILES, j=GROUP)
                dve.wait_ge(c.oa_turned, nth(b, GROUPS, g + 1))
                dve.reciprocal(c.inv_a[:], o[:, :, :, HD_A]).then_inc(c.oa_inv, 1)
                dve.wait_ge(c.oa_inv, nth(b, GROUPS, g + 1))
                if g == 0:
                    dve.wait_ge(c.at_turned, nth(b, 1, 0))
                dve.tensor_tensor(c.a_tok[:, :, at:at + BLK].rearrange("p t (j d) -> p t j d", j=GROUP),
                                  o[:, :, :, 0:HD_A],
                                  c.inv_a[:].rearrange("p t (j a) -> p t j a", a=1)
                                  .broadcast_to([P, TILES, GROUP, HD_A]), ALU.mult).then_inc(c.oa_tok, 1)

            def keep_values(b):
                dve.wait_ge(c.va_ps, nth(b, 1, 1))
                dve.wait_ge(c.oa_ps, nth(b, GROUPS, 0))
                dve.tensor_tensor(c.v_a[:, :, :, 0:HD_A],
                                  ps[:, 7, :].rearrange("p (t h d) -> p t h d", t=TILES, h=HEADS),
                                  c.bva[:].rearrange("p (a h d) -> p a h d", a=1, h=HEADS)
                                  .broadcast_to([P, TILES, HEADS, HD_A]), ALU.add).then_inc(c.va_ok, 1)

            def add_output(b):
                dve.wait_ge(c.woa_ps, nth(b, 1, 0))
                dve.wait_ge(c.x_bias, nth(b, 1, 0))
                x_b = c.x_res[:, bass.ds((b - 1) * TILES, TILES), :]
                dve.tensor_tensor(x_b, ps[:, 7, :].rearrange("p (t d) -> p t d", t=TILES), x_b, ALU.add)\
                   .then_inc(c.a_added, 1)

            def input_low(b):
                dve.wait_ge(c.xn_hi_ok, b + 1)
                dve.tensor_tensor(c.xn_lo[:], ps[:, 7, :], c.xn_hi[:].bitcast(F32), ALU.subtract)\
                   .then_inc(c.xn_lo_ok, 1)

            raw_ka, raw_qa, raw_va = raw_weights(c)
            dve.wait_ge(c.x0_loaded, 16)
            ln_statistics(c, dve, 0, 0)
            dve.wait_ge(c.ka_loaded, 16)
            split_weights(c, dve, c.wka_hi[:], c.wka_lo[:], raw_ka, 1)
            dve.wait_ge(c.qa_loaded, 16)
            split_weights(c, dve, c.wqa_hi[:], c.wqa_lo[:], raw_qa, 2)
            ln_normalise(c, dve, 0, 0)
            dve.wait_ge(c.va_loaded, 16)
            split_weights(c, dve, c.wva_hi[:], c.wva_lo[:], raw_va, 3)
            input_low(0)
            dve.wait_ge(c.bias_loaded, 3 * 16)
            k_low(-1, 4)
            mask_keys(-1, 4)
            q_low(-1, 4, bank=6)
            dve.wait_ge(c.x_loaded, (B - 1) * 16)
            dve.wait_ge(c.bva_loaded, 16)
            dve.wait_ge(c.set_const, 7)

            def batch(b, prev, own, more):
                if not own:
                    dve.wait_ge(c.later_loaded, 8 * 16)
                    dve.wait_ge(c.wb_low, 3)
                    mix.statistics(dve, 0)
                    divide(b, -3)
                    mix.vector(dve, 0, prev=False)
                    divide(b, -2)
                    mix.vector(dve, 1)
                    mix.vector(dve, 2, more=False)
                    divide(b, -1)
                    add_output(b)
                    return
                for s in range(GROUPS):
                    following = s < 3 or more
                    for i in range(16):
                        maximum(b, s, i)
                        if i == (7 if s == 3 else 5) and (prev or s == 3):
                            divide(b, s - 3)
                        if i == (11 if s == 3 else 8) and following:
                            k_low(b, s + 1)
                        if s < 3 and i == 13:
                            q_low(b, s + 1)
                            mask_keys(b, s + 1)
                        if prev and s == 3 and i == 0:
                            add_output(b)
                        if more and s == 2 and i == 13:
                            ln_statistics(c, dve, 0, b + 1)
                        if more and s == 3 and i == 1:
                            ln_normalise(c, dve, 0, b + 1)
                        if more and s == 3 and i == 5:
                            input_low(b + 1)
                    if more and s == 3:
                        q_low(b, s + 1)
                        mask_keys(b, s + 1)
                    split_maxima(b, s)
                    if s == 1:
                        keep_values(b)

            each_batch(dve, batch)

        @block.scalar
        def _(act):
            def k_high(b, g):
                act.wait_ge(c.ka_ps, nth(b, GROUPS, g + 1))
                act.wait_ge(c.km_dve, nth(b, GROUPS, g))
                act.wait_ge(c.km_act, nth(b, HEADS - GROUPS, (GROUP - 1) * g))
                act.activation(c.k_group[:], ps[:, 7, :], ACT.Identity,
                               bias=c.bka[:, g % GROUPS:g % GROUPS + 1])\
                   .then_inc(c.ka_hi, 1)

            def q_high(b, g, bank=7):
                act.wait_ge(c.qa_ps, nth(b, GROUPS, g + 1))
                act.wait_ge(c.t_ps, nth(b, HALVES, 8 * (g - GROUPS) + 8))
                act.activation(q_stack(g), ps[:, bank, :], ACT.Identity,
                               bias=c.bqa[:, g % GROUPS:g % GROUPS + 1])\
                   .then_inc(c.qa_hi, 1)

            def mask_keys(b, g, j):
                act.wait_ge(c.ka_lo, nth(b, GROUPS, g + 1))
                act.wait_ge(c.t_ps, nth(b, HALVES, 8 * (g - 2) + 2 * j + 2))
                act.activation(k_stack(g, j), c.k_group[:].bitcast(F32), ACT.Copy, scale=c.head_mask[:, j:j + 1])\
                   .then_inc(c.km_act, 1)

            def set_maxima(b, g):
                act.wait_ge(c.m_turned, nth(b, GROUPS, g + 1))
                act.activation(c.q_stack[M_ROWS:P, g % GROUPS, :], ps[0:BLK, 7, :], ACT.Copy).then_inc(c.m_set, 1)

            def exponentials(b, g, n):
                half = 8 * g + n
                act.wait_ge(c.t_ps, nth(b, HALVES, half + 1))
                if n == 0:
                    act.wait_ge(c.oa_ps, nth(b, GROUPS, g - 1))
                at = 2 + 2 * (half % 2)
                col = 2 * (n % 2) * S
                act.activation(probs(g, n // 2)[:, col:col + 2 * S].rearrange("p (k n) -> p k n", k=2),
                               ps[:, at:at + 2, :], ACT.Exp, scale=SCALE_A).then_inc(c.t_exp, 1)

            def keep_output(b, g):
                act.wait_ge(c.oa_ps, nth(b, GROUPS, g + 1))
                act.wait_ge(c.oa_turned, nth(b, GROUPS, g))
                act.activation(c.o_sb[:], ps[:, 6, :], ACT.Copy).then_inc(c.oa_sb, 1)

            def keep_turned(b):
                act.wait_ge(c.at_turned, nth(b, 1, 0))
                act.activation(c.a_chan[:], ps[:, 7, :], ACT.Copy).then_inc(c.at_sb, 1)

            def input_high(b):
                act.wait_ge(c.ln_turned, b + 1)
                act.wait_ge(c.qa_ps, nth(b, GROUPS, 0))
                act.wait_ge(c.va_ps, nth(b, 1, 0))
                act.activation(c.xn_hi[:], ps[:, 7, :], ACT.Copy).then_inc(c.xn_hi_ok, 1)

            first_loads_scalar(c, act, d)

            input_high(0)
            act.wait_ge(c.set_const, 7)
            act.wait_ge(c.bias_loaded, 3 * 16)
            k_high(-1, 4)
            q_high(-1, 4, bank=6)
            mask_keys(-1, 4, 1)

            def batch(b, prev, own, more):
                if not own:
                    act.wait_ge(c.wb_low, 3)
                for s in range(GROUPS if own else GROUPS - 1):
                    following = own and (s < 3 or more)
                    before = own if s >= 2 else prev
                    last = own if s >= 1 else prev
                    if before:
                        exponentials(b, s - 2, 6)
                    if last:
                        set_maxima(b, s - 1)
                    if before:
                        exponentials(b, s - 2, 7)
                    for n in range(6):
                        if own and n < 2:
                            mask_keys(b, s, n + 2)
                        if last:
                            exponentials(b, s - 1, n)
                        if not own and (s, n) in ((0, 1), (1, 1), (1, 5)):
                            mix.keep_input(act, s if n == 1 else 2)
                        if not own and (s, n) in ((0, 4), (1, 3)):
                            mix.activations(act, s)
                        if following and s == 3 and n == 0:
                            input_high(b + 1)
                        if following and n == (3 if s == 3 else 1):
                            k_high(b, s + 1)
                        if following and n == (4 if s == 3 else 3):
                            q_high(b, s + 1)
                    if not own and s == 2:
                        mix.activations(act, 2)
                    if prev and s == 2:
                        keep_turned(b)
                    if following:
                        mask_keys(b, s + 1, 1)
                    if before:
                        keep_output(b, s - 2)

            each_batch(act, batch)

        @block.sync
        def _(sp):
            first_loads_sync(c, sp, d)
            later_loads(c, sp, d)

        @block.gpsimd
        def _(pool):
            set_constants(c, pool)
            ln_pool(c, pool, 0, 0)
            pool.wait_ge(c.boa_loaded, 16)
            add_bias(c, pool, 0, 0, c.boa)
            split_later_weights(c, pool)

            def batch(b, prev, own, more):
                if not own:
                    for s in range(3):
                        mix.pool(pool, s)
                if more:
                    ln_pool(c, pool, 0, b + 1)
                    add_bias(c, pool, 0, b + 1, c.boa)

            each_batch(pool, batch)


def attention_b(c, out):
    nc, ps = c.nc, c.ps
    SCORES = PAIRS * TILES
    mix = Mixing(c, 1)
    before, last = Mixing(c, 0), B - 1
    flat = c.probs[:].rearrange("p s n -> p (s n)")

    def part(p, which):
        return c.stack[:, 4 * (p % 2) + which, :]

    def p_at(p, a):
        at = (2 * (p % 2) + a) * CAUSAL
        return flat[:, at:at + CAUSAL]

    def pt_at(p, a):
        at = (4 + 2 * (p % 2) + a) * CAUSAL
        return flat[:, at:at + CAUSAL]

    def out_at(p):
        at = 8 * CAUSAL + (p % PAIRS) * S
        return flat[:, at:at + S]

    def unit_columns(u):
        return COL_AT[UNITS[u][0]], sum(TILES - k for k in UNITS[u]) * P

    def unit_bank(a, u):
        return 4 + (3 * a + u) % 2

    VALUE_STEPS = (0, 1, 3, 4)

    def values_before_step(p):
        return 2 * sum(1 for v in VALUE_STEPS if v < p)

    def values_for(p):
        return 0 if p < 0 else TILES if p < PAIRS // 2 else 2 * TILES

    def value_tile(n):
        return n % TILES, n // TILES

    with nc.Block() as block:
        @block.tensor
        def _(pe):
            def project(p, which, bank, done):
                col = which * HEADS * HD_B + (p % PAIRS) * P
                three_passes(pe, ps[:, bank, :], (c.wb_hi[:, col:col + P], c.wb_lo[:, col:col + P]),
                             (c.xn_hi[:], c.xn_lo[:])).then_inc(done, 1)

            def scores(b, p, i):
                w = (i + 1) * P
                q = slice(i * P, (i + 1) * P)
                if i == 0:
                    pe.wait_ge(c.qb_lo, nth(b, PAIRS, p + 1))
                    pe.wait_ge(c.kb_lo, nth(b, PAIRS, p + 1))
                pe.wait_ge(c.s_exp, nth(b, 2 * SCORES, 8 * p + 2 * i - 2))
                for q_part, k_part in ((0, 2), (1, 2), (0, 3)):
                    for a in range(2):
                        rows = slice(HD_B * a, HD_B * (a + 1))
                        pe.matmul(ps[:, 2 * (i % 2) + a, 0:w], part(p, q_part)[rows, q], part(p, k_part)[rows, 0:w],
                                  start=(q_part, k_part) == (0, 2), stop=False)
                for a in range(2):
                    mm = pe.matmul(ps[:, 2 * (i % 2) + a, i * P:w], c.ident_bf[:], c.causal_bf[:],
                                   start=False, stop=True)
                mm.then_inc(c.s_ps, 1)

            def turn(b, p, a, u):
                if u == 0:
                    pe.wait_ge(c.s_exp, nth(b, 2 * SCORES, 8 * p + 7 + a))
                if a == 0 and u < 2:
                    if p in VALUE_STEPS:
                        pe.wait_ge(c.vb_ok, nth(b, 2 * TILES, values_before_step(p + 1) - 1 + u))
                    if p == 2:
                        pe.wait_ge(c.b_added, nth(b, TILES, u - 1))
                if (a, u) in ((0, 2), (1, 2)):
                    pe.wait_ge(c.xp_act, nth(b, HEADS, 2 * p + a + 1))
                elif a == 0:
                    pe.wait_ge(c.xp_dve, nth(b, 2 * HEADS, 4 * (p - 1) + 3 + u))
                else:
                    pe.wait_ge(c.xp_dve, nth(b, 2 * HEADS, 4 * p + 1 + u))
                col = 0
                for kt in UNITS[u]:
                    for qt in range(kt, TILES):
                        at = ROW_AT[qt] + kt * P
                        mm = pe.transpose(ps[:, unit_bank(a, u), col:col + P], p_at(p, a)[:, at:at + P], c.ident[:])
                        col += P
                mm.then_inc(c.xp_ps, 1)

            def turn_reciprocals(b, p):
                pe.wait_ge(c.inv_sb, nth(b, PAIRS, p))
                pe.wait_ge(c.wide_ok, nth(b, PAIRS, p + 1))
                for qt in range(TILES):
                    mm = pe.transpose(ps[:, 7, qt * P:(qt + 1) * P],
                                      c.inv_wide[:, qt, :, :].rearrange("p a d -> p (a d)"), c.ident[:])
                mm.then_inc(c.inv_turned, 1)

            def times_values(b, p, kt):
                if kt == 0:
                    pe.wait_ge(c.vb_ok, nth(b, 2 * TILES, values_for(p)))
                    pe.wait_ge(c.ob_sb, nth(b, PAIRS, p))
                    pe.wait_ge(c.xp_act, nth(b, HEADS, 2 * p + 2))
                    pe.wait_ge(c.xp_dve, nth(b, 2 * HEADS, 4 * p + 4))
                w = (TILES - kt) * P
                for a in range(2):
                    h = (2 * p + a) % HEADS
                    mm = pe.matmul(ps[HD_B * a:HD_B * (a + 1), 6, kt * P:S], c.v_b[:, kt, h * HD_B:(h + 1) * HD_B],
                                   pt_at(p, a)[:, COL_AT[kt]:COL_AT[kt] + w],
                                   start=(kt == 0), stop=(kt == TILES - 1))
                if kt == TILES - 1:
                    mm.then_inc(c.ob_ps, 1)

            def project_values(b, p, n):
                t, half = value_tile(n)
                tok = slice(t * P, (t + 1) * P)
                col = 2 * HEADS * HD_B + half * S
                pe.wait_ge(c.xp_dve, nth(b, 2 * HEADS, 4 * (p - 1) + 3 + n % 2))
                three_passes(pe, ps[:, 4 + n % 2, :], (c.xn_hi[:, tok], c.xn_lo[:, tok]),
                             (c.wb_hi[:, col:col + S], c.wb_lo[:, col:col + S])).then_inc(c.vb_ps, 1)

            def output_product(b, t, own):
                if t == 0:
                    pe.wait_ge(c.ob_sb, nth(b, PAIRS, 0))
                if t < 2:
                    pe.wait_ge(c.xp_dve, nth(b, 2 * HEADS, 7 + t if own else 0))
                else:
                    pe.wait_ge(c.b_added, nth(b, TILES, t - 5))
                for p in range(PAIRS):
                    mm = pe.matmul(ps[:, 4 + t % 2, 0:P], out_at(p)[:, t * P:(t + 1) * P],
                                   c.wob[:, p, :], start=(p == 0), stop=(p == PAIRS - 1))
                mm.then_inc(c.wob_ps, 1)

            def step(b, p, prev, own, more):
                turns = own if p >= 1 else prev
                values = own if p >= 2 else prev
                following = own and p + 1 < PAIRS
                ahead = more and p + 1 == PAIRS
                if own:
                    scores(b, p, 0)
                if following or ahead:
                    pe.wait_ge(c.inv_sb, nth(b, PAIRS, p - 2))
                    pe.wait_ge(c.kb_lo, nth(b, PAIRS, p + 1))
                if following:
                    project(p + 1, 0, 7, c.qb_ps)
                if ahead:
                    ln_tensor(c, pe, 2, b + 1, 7)
                if turns:
                    turn(b, p - 1, 0, 0)
                    turn(b, p - 1, 0, 1)
                if own:
                    scores(b, p, 1)
                if values:
                    times_values(b, p - 2, 0)
                if turns:
                    turn(b, p - 1, 0, 2)
                if following:
                    pe.wait_ge(c.qb_lo, nth(b, PAIRS, p + 2))
                    project(p + 1, 1, 7, c.kb_ps)
                if ahead:
                    pe.wait_ge(c.xn_lo_ok, B + b + 2)
                    project(p + 1, 0, 7, c.qb_ps)
                if own:
                    scores(b, p, 2)
                if turns:
                    turn(b, p - 1, 1, 0)
                    turn(b, p - 1, 1, 1)
                if values:
                    times_values(b, p - 2, 1)
                if ahead:
                    pe.wait_ge(c.qb_lo, nth(b, PAIRS, p + 2))
                    project(p + 1, 1, 7, c.kb_ps)
                if own:
                    scores(b, p, 3)
                if values and not ahead:
                    if own:
                        pe.wait_ge(c.kb_lo, nth(b, PAIRS, min(p + 2, PAIRS)))
                    turn_reciprocals(b, p - 2)
                if turns:
                    turn(b, p - 1, 1, 2)
                if values:
                    times_values(b, p - 2, 2)
                    times_values(b, p - 2, 3)
                if ahead:
                    pe.wait_ge(c.kb_lo, nth(b, PAIRS, p + 2))
                    turn_reciprocals(b, p - 2)
                if own and p in VALUE_STEPS:
                    for n in (0, 1):
                        project_values(b, p, values_before_step(p) + n)
                if own and prev and p == 2:
                    for t in range(TILES):
                        output_product(b, t, own)

            before.norm_and_value(pe, last)
            before.key_and_receptance(pe, last)

            ln_tensor(c, pe, 2, 0, 7)
            before.norm_and_value(pe, B, own=False)
            pe.wait_ge(c.xn_lo_ok, B + 1)
            project(PAIRS, 0, 7, c.qb_ps)
            project(PAIRS, 1, 6, c.kb_ps)
            pe.wait_ge(c.gated_ok, B)

            def finish(b):
                step(b, 0, True, False, False)
                mix.norm_and_value(pe, 0, prev=False)
                times_values(b, -1, 0)
                times_values(b, -1, 1)
                turn_reciprocals(b, -1)
                times_values(b, -1, 2)
                times_values(b, -1, 3)
                mix.key_and_receptance(pe, 0)
                mix.norm_and_value(pe, 1)
                output_product(b, 0, False)
                mix.key_and_receptance(pe, 1)
                output_product(b, 1, False)
                mix.norm_and_value(pe, 2)
                output_product(b, 2, False)
                mix.key_and_receptance(pe, 2)
                output_product(b, 3, False)

            def batch(b, prev, own, more):
                if not own:
                    finish(b)
                    return
                for p in range(PAIRS):
                    step(b, p, prev, own, more)

            each_batch(pe, batch)

        @block.vector
        def _(dve):
            def low(b, p, which, hi_ready, done, bank=7):
                dve.wait_ge(hi_ready, nth(b, PAIRS, p + 1))
                dve.scalar_tensor_tensor(out=part(p, 2 * which + 1), in0=ps[:, bank, :],
                                         scalar=c.bqkb[:, which, p % PAIRS:p % PAIRS + 1],
                                         in1=part(p, 2 * which).bitcast(F32),
                                         op0=ALU.add, op1=ALU.subtract).then_inc(done, 1)

            def maxima(b, p, i):
                n = TILES * p + i
                at = 2 * (i % 2)
                dve.wait_ge(c.s_ps, nth(b, SCORES, n + 1))
                if i == 0:
                    dve.wait_ge(c.s_exp, nth(b, 2 * SCORES, 8 * (p - 7)))
                dve.tensor_reduce(c.neg_max_b[:, 2 * p:2 * p + 2, i], ps[:, at:at + 2, 0:(i + 1) * P], AX_X,
                                  ALU.max, negate=True).then_inc(c.s_max, 1)

            def copy_turned(b, p, a, u):
                col, w = unit_columns(u)
                dve.wait_ge(c.xp_ps, nth(b, 3 * HEADS, 6 * p + 3 * a + u + 1))
                dve.wait_ge(c.ob_ps, nth(b, PAIRS, p - 1))
                dve.tensor_copy(pt_at(p, a)[:, col:col + w], ps[:, unit_bank(a, u), 0:w]).then_inc(c.xp_dve, 1)

            def reciprocals(b, p):
                heads = slice((2 * p) % HEADS, (2 * p) % HEADS + 2)
                dve.wait_ge(c.s_exp, nth(b, 2 * SCORES, 8 * p + 8))
                dve.wait_ge(c.wide_ok, nth(b, PAIRS, p))
                dve.tensor_tensor(c.den_b[:], c.sum_b[:, heads, :],
                                  c.ghost[:, heads].rearrange("p (a b) -> p a b", b=1)
                                  .broadcast_to([P, 2, TILES]), ALU.add).then_inc(c.den_ok, 1)
                dve.wait_ge(c.den_ok, nth(b, PAIRS, p + 1))
                dve.reciprocal(c.inv_b[:], c.den_b[:]).then_inc(c.inv_ok, 1)

            def finish(b, p):
                dve.wait_ge(c.ob_ps, nth(b, PAIRS, p + 1))
                dve.wait_ge(c.inv_sb, nth(b, PAIRS, p + 1))
                if p == 0:
                    dve.wait_ge(c.wob_ps, nth(b, TILES, 0))
                dve.tensor_tensor(out_at(p), ps[:, 6, :], c.inv_chan[:], ALU.mult).then_inc(c.ob_sb, 1)

            def keep_values(b, n):
                kt, half = value_tile(n)
                dve.wait_ge(c.vb_ps, nth(b, 2 * TILES, n + 1))
                dve.wait_ge(c.ob_ps, nth(b, PAIRS, 0 if half else -PAIRS // 2))
                dve.tensor_tensor(c.v_b[:, kt, half * S:(half + 1) * S], ps[:, 4 + n % 2, :],
                                  c.bvb[:, half * S:(half + 1) * S], ALU.add).then_inc(c.vb_ok, 1)

            def add_output(b, t):
                dve.wait_ge(c.wob_ps, nth(b, TILES, t - 3))
                dve.wait_ge(c.x_bias, B + b)
                x_t = c.x_res[:, bass.ds((b - 1) * TILES + t, 1), :].rearrange("p a d -> p (a d)")
                dve.tensor_tensor(x_t, ps[:, 4 + t % 2, 0:P], x_t, ALU.add).then_inc(c.b_added, 1)

            def input_low(b):
                dve.wait_ge(c.xn_hi_ok, B + b + 1)
                dve.tensor_tensor(c.xn_lo[:], ps[:, 7, :], c.xn_hi[:].bitcast(F32), ALU.subtract)\
                   .then_inc(c.xn_lo_ok, 1)

            def step(b, p, prev, own, more):
                turns = own if p >= 1 else prev
                following = own and p + 1 < PAIRS
                ahead = more and p + 1 == PAIRS
                if own:
                    maxima(b, p, 0)
                if own if p >= 3 else prev:
                    finish(b, p - 3)
                if following:
                    low(b, p + 1, 0, c.qb_hi, c.qb_lo)
                if turns:
                    copy_turned(b, p - 1, 0, 1)
                if ahead:
                    input_low(b + 1)
                if own:
                    maxima(b, p, 1)
                if turns:
                    copy_turned(b, p - 1, 0, 2)
                    reciprocals(b, p - 1)
                if more and p + 2 == PAIRS:
                    dve.wait_ge(c.f_added, B)
                    ln_statistics(c, dve, 2, b + 1)
                if own:
                    maxima(b, p, 2)
                if following:
                    low(b, p + 1, 1, c.kb_hi, c.kb_lo)
                if ahead:
                    low(b, p + 1, 0, c.qb_hi, c.qb_lo)
                if turns:
                    copy_turned(b, p - 1, 1, 1)
                if ahead:
                    low(b, p + 1, 1, c.kb_hi, c.kb_lo)
                if own:
                    maxima(b, p, 3)
                if turns:
                    copy_turned(b, p - 1, 1, 2)
                if more and p + 2 == PAIRS:
                    ln_normalise(c, dve, 2, b + 1)
                if own and p in VALUE_STEPS:
                    for n in (0, 1):
                        keep_values(b, values_before_step(p) + n)
                if prev and p == 2:
                    for t in range(TILES):
                        add_output(b, t)

            before.statistics(dve, last)
            before.vector(dve, last, more=False)
            dve.wait_ge(c.f_added, 1)
            ln_statistics(c, dve, 2, 0)
            ln_normalise(c, dve, 2, 0)
            before.vector(dve, B, own=False, more=False)
            input_low(0)
            low(-1, PAIRS, 0, c.qb_hi, c.qb_lo)
            low(-1, PAIRS, 1, c.kb_hi, c.kb_lo, bank=6)

            def last_steps(b):
                finish(b, -3)
                copy_turned(b, -1, 0, 1)
                mix.statistics(dve, 0)
                copy_turned(b, -1, 0, 2)
                reciprocals(b, -1)
                copy_turned(b, -1, 1, 1)
                copy_turned(b, -1, 1, 2)
                finish(b, -2)
                mix.vector(dve, 0, prev=False)
                finish(b, -1)
                mix.vector(dve, 1)
                add_output(b, 0)
                mix.vector(dve, 2, more=False)
                for t in range(1, TILES):
                    add_output(b, t)

            def batch(b, prev, own, more):
                if not own:
                    last_steps(b)
                    return
                for p in range(PAIRS):
                    step(b, p, prev, own, more)

            each_batch(dve, batch)

        @block.scalar
        def _(act):
            def high(b, p, which, ps_ready, done, bank=7):
                act.wait_ge(ps_ready, nth(b, PAIRS, p + 1))
                act.wait_ge(c.s_ps, nth(b, SCORES, TILES * (p - 1)))
                act.activation(part(p, 2 * which), ps[:, bank, :], ACT.Identity,
                               bias=c.bqkb[:, which, p % PAIRS:p % PAIRS + 1]).then_inc(done, 1)

            def exponentials(b, p, i):
                w = (i + 1) * P
                act.wait_ge(c.s_max, nth(b, SCORES, TILES * p + i + 1))
                if i == 0:
                    act.wait_ge(c.xp_ps, nth(b, 3 * HEADS, 6 * (p - 1)))
                    act.wait_ge(c.den_ok, nth(b, PAIRS, p - 4))
                for a in range(2):
                    h = 2 * p + a
                    act.activation(p_at(p, a)[:, ROW_AT[i]:ROW_AT[i] + w], ps[:, 2 * (i % 2) + a, 0:w], ACT.Exp,
                                   bias=c.neg_max_b[:, h, i:i + 1], accum_out=c.sum_b[:, h, i:i + 1])\
                       .then_inc(c.s_exp, 1)

            def copy_turned(b, p, a):
                act.wait_ge(c.xp_ps, nth(b, 3 * HEADS, 6 * p + 3 * a + 1))
                act.wait_ge(c.ob_ps, nth(b, PAIRS, p - 1))
                act.activation(pt_at(p, a)[:, 0:S], ps[:, unit_bank(a, 0), :], ACT.Copy).then_inc(c.xp_act, 1)

            def reciprocal_rows(b, p):
                act.wait_ge(c.inv_turned, nth(b, PAIRS, p + 1))
                act.wait_ge(c.ob_sb, nth(b, PAIRS, p))
                act.activation(c.inv_chan[:], ps[:, 7, :], ACT.Copy).then_inc(c.inv_sb, 1)

            def input_high(b):
                act.wait_ge(c.ln_turned, 2 * B + b + 1)
                act.wait_ge(c.vb_ps, nth(b, 2 * TILES, 0))
                act.wait_ge(c.kb_ps, nth(b, PAIRS, 0))
                act.activation(c.xn_hi[:], ps[:, 7, :], ACT.Copy).then_inc(c.xn_hi_ok, 1)

            def step(b, p, prev, own, more):
                turns = own if p >= 1 else prev
                values = own if p >= 2 else prev
                following = own and p + 1 < PAIRS
                ahead = more and p + 1 == PAIRS
                if own:
                    exponentials(b, p, 0)
                if following:
                    high(b, p + 1, 0, c.qb_ps, c.qb_hi)
                if ahead:
                    input_high(b + 1)
                if turns:
                    copy_turned(b, p - 1, 0)
                if own:
                    exponentials(b, p, 1)
                if following:
                    high(b, p + 1, 1, c.kb_ps, c.kb_hi)
                if ahead:
                    high(b, p + 1, 0, c.qb_ps, c.qb_hi)
                if turns:
                    copy_turned(b, p - 1, 1)
                if own:
                    exponentials(b, p, 2)
                if values and not ahead:
                    reciprocal_rows(b, p - 2)
                if ahead:
                    high(b, p + 1, 1, c.kb_ps, c.kb_hi)
                if own:
                    exponentials(b, p, 3)
                if ahead:
                    reciprocal_rows(b, p - 2)

            before.keep_input(act, last)
            before.activations(act, last)
            input_high(0)
            high(-1, PAIRS, 0, c.qb_ps, c.qb_hi)
            high(-1, PAIRS, 1, c.kb_ps, c.kb_hi, bank=6)

            def last_steps(b):
                copy_turned(b, -1, 0)
                copy_turned(b, -1, 1)
                reciprocal_rows(b, -2)
                mix.keep_input(act, 0)
                reciprocal_rows(b, -1)
                mix.activations(act, 0)
                for n in (1, 2):
                    mix.keep_input(act, n)
                    mix.activations(act, n)

            def batch(b, prev, own, more):
                if not own:
                    last_steps(b)
                    return
                for p in range(PAIRS):
                    step(b, p, prev, own, more)

            each_batch(act, batch)

        @block.sync
        def _(sp):
            mix.store(sp, out, (0, 1))

        @block.gpsimd
        def _(pool):
            def widen(b, p):
                pool.wait_ge(c.inv_ok, nth(b, PAIRS, p + 1))
                pool.wait_ge(c.inv_turned, nth(b, PAIRS, p))
                pool.tensor_tensor(c.inv_wide[:], c.inv_b[:].rearrange("p a (t d) -> p t a d", d=1)
                                   .broadcast_to([P, TILES, 2, HD_B]),
                                   c.zero[:].rearrange("p (a b d) -> p a b d", a=1, b=1)
                                   .broadcast_to([P, TILES, 2, HD_B]), ALU.add).then_inc(c.wide_ok, 1)

            before.pool(pool, last)
            ln_pool(c, pool, 2, 0)
            add_bias(c, pool, 2, 0, c.bob)

            def batch(b, prev, own, more):
                if not own:
                    mix.pool(pool, 0)
                if prev:
                    widen(b, -1)
                if not own:
                    mix.pool(pool, 1)
                    mix.pool(pool, 2)
                if own:
                    for p in range(PAIRS - 1):
                        if more and p == PAIRS - 3:
                            ln_pool(c, pool, 2, b + 1)
                        widen(b, p)
                if more:
                    add_bias(c, pool, 2, b + 1, c.bob)

            each_batch(pool, batch)


def build(nc, d, out):
    with ExitStack() as ctx:
        c = Chip(nc, ctx)
        memory(c)
        semaphores(c)
        attention_a(c, d)
        attention_b(c, out)
        last_mixing(c, 1, out)


def kernel(**inputs):
    import numpy as np
    import concourse.bacc as bacc
    from concourse.bass_utils import run_bass_kernel_spmd

    a = {k: np.asarray(v) for k, v in inputs.items()}

    def stacked(w):
        t = w.T.reshape(P, GROUPS, BLK)
        return np.concatenate([t, t, t, np.zeros_like(t)], axis=2)

    def stacked_bias(v, fill):
        t = v.reshape(GROUPS, BLK).T
        return np.concatenate([t, t, t, np.full_like(t, fill)], axis=0)

    rows = np.arange(P)
    block, at = rows // BLK, rows % BLK
    head_mask = np.stack([np.where(block < 3, at // HD_A == j, at // 2 == j) for j in range(GROUP)], axis=1)
    causal = np.where(rows[None, :] > rows[:, None], -1e30, 0.0)
    arrays = {
        "x": a["L0_attn_a_x"],
        "wqa": stacked(a["L0_attn_a_Wq"]), "wka": stacked(a["L0_attn_a_Wk"]),
        "wva": a["L0_attn_a_Wv"].T, "woa": a["L0_attn_a_Wo"].T,
        "bqa": stacked_bias(a["L0_attn_a_bq"], 0.0), "bka": stacked_bias(a["L0_attn_a_bk"], 1.0),
        "bva": a["L0_attn_a_bv"], "boa": a["L0_attn_a_bo"],
        "wb": a["L0_attn_b_Wqkv_w"].T, "wob": a["L0_attn_b_Wo_w"].T,
        "bqkb": a["L0_attn_b_Wqkv_b"][:2 * HEADS * HD_B].reshape(2, PAIRS, P).transpose(2, 0, 1),
        "bvb": a["L0_attn_b_Wqkv_b"][2 * HEADS * HD_B:], "bob": a["L0_attn_b_Wo_b"],
        "ghost": a["L0_attn_b_ghost"],
        "wr": a["L0_ffn_W_r"].T, "wk": a["L0_ffn_W_k"].T, "wv": a["L0_ffn_W_v"].T,
        "mu": np.stack([a["L0_ffn_mu_r"], a["L0_ffn_mu_k"]], axis=1),
        "ident": np.eye(P, dtype=np.float32), "head_mask": head_mask.astype(np.float32),
        "causal": causal.astype(np.float32),
    }
    arrays = {k: np.ascontiguousarray(v) for k, v in arrays.items()}

    nc = bacc.Bacc("TRN2", target_bir_lowering=False, num_devices=1)
    d = {k: nc.dram_tensor("in_" + k, v.shape, mybir.dt.from_np(v.dtype), kind="ExternalInput").ap()
         for k, v in arrays.items()}
    out = nc.dram_tensor("out", (B, S, P), F32, kind="ExternalOutput").ap()
    build(nc, d, out)
    r = run_bass_kernel_spmd(nc, [{"in_" + k: v for k, v in arrays.items()}], core_ids=[0])
    return r.results[0]["out"]
```
